# Optimizing a Trainium2 kernel written in Bass

```python
import numpy as np
import jax
import jax.numpy as jnp

def _softmax(x, axis=-1):
    return jax.nn.softmax(x, axis=axis)

def _gelu(x):
    return jax.nn.gelu(x, approximate=True)

def _silu(x):
    return jax.nn.silu(x)

def _sigmoid(x):
    return jax.nn.sigmoid(x)

def _layernorm(x, axis=-1, eps=1e-05):
    m = jnp.mean(x, axis=axis, keepdims=True)
    v = jnp.var(x, axis=axis, keepdims=True)
    return (x - m) / jnp.sqrt(v + eps)

def _scatter_add(tgt, idx, src, axis=0):
    return tgt.at[idx].add(src)

def _segment_sum(src, seg, n):
    return jax.ops.segment_sum(src, seg, n)
kernel_name = 'mk_flamingo_gated_d4_seqx_r8_f56283'

def setup_inputs(seed: int=0):
    np.random.seed(seed)
    _w = jnp.asarray

    def _rec_inputs():
        import jax
        import jax.numpy as jnp
        _rk = jax.random.key(seed)
        x = -0.0003929 + 0.9999 * jax.random.normal(jax.random.fold_in(_rk, 1), (4, 512, 128), jnp.float32)
        _lenS = 512 - jax.random.randint(jax.random.fold_in(_rk, 7), (4,), 0, max(1, 512 // 4) + 1, jnp.int32)
        _lenS2 = 77 - jax.random.randint(jax.random.fold_in(_rk, 8), (4,), 0, max(1, 77 // 4) + 1, jnp.int32)
        _ctx_512P = jax.random.normal(jax.random.fold_in(_rk, 11), (4, 16, 64), jnp.float32)
        _ctx_512c = jax.random.dirichlet(jax.random.fold_in(_rk, 511), 0.3 * jnp.ones((16,), jnp.float32), (4, 77))
        _ctx_512t = jnp.einsum('bsk,bkd->bsd', _ctx_512c, _ctx_512P)
        _ctx_512t = _ctx_512t * jax.lax.rsqrt(jnp.mean(jnp.square(_ctx_512t)) + 1e-12) * 0.953939
        ctx_512 = -1.39393e-06 + 0.999914 * (_ctx_512t + 0.3 * jax.random.normal(jax.random.fold_in(_rk, 611), (4, 77, 64), jnp.float32))
        _g = jax.random.normal(jax.random.fold_in(_rk, 9001), (2, 4), jnp.float32)
        _g = jnp.sign(_g) * jnp.maximum(jnp.abs(_g), 1.0) + (_g == 0) * 1.0
        g_xattn = _g[0]
        g_ffn = _g[1]
        return (x, ctx_512, g_xattn, g_ffn)
    x, ctx_512, g_xattn, g_ffn = _rec_inputs()

    def _L0_xattn_setup():
        import jax, jax.numpy as jnp
        import numpy as np
        HEADS = 16
        D_MODEL = 128
        IMG_MODEL = 64
        D_K = D_MODEL // HEADS
        key = jax.random.key(seed)
        ks = jax.random.split(key, 12)
        B, LQ, LKV = (8, 256, 128)
        s_dm = 1.0 / np.sqrt(D_MODEL)
        s_im = 1.0 / np.sqrt(IMG_MODEL)
        return {'q': jax.random.normal(ks[0], (B, LQ, D_MODEL), jnp.float32), 'k': jax.random.normal(ks[1], (B, LKV, IMG_MODEL), jnp.float32), 'v': jax.random.normal(ks[2], (B, LKV, IMG_MODEL), jnp.float32), 'Wq': jax.random.normal(ks[3], (D_MODEL, D_MODEL), jnp.float32) * s_dm, 'bq': jnp.zeros((D_MODEL,), jnp.float32), 'Wk': jax.random.normal(ks[4], (IMG_MODEL, D_MODEL), jnp.float32) * s_im, 'bk': jnp.zeros((D_MODEL,), jnp.float32), 'Wv': jax.random.normal(ks[5], (IMG_MODEL, D_MODEL), jnp.float32) * s_im, 'bv': jnp.zeros((D_MODEL,), jnp.float32), 'Wo': jax.random.normal(ks[6], (D_MODEL, D_MODEL), jnp.float32) * s_dm, 'bo': jnp.zeros((D_MODEL,), jnp.float32)}
    _L0_xattn_all = _L0_xattn_setup()
    _L0_xattn_in = {k: v for k, v in _L0_xattn_all.items() if k in ('Wq', 'bq', 'Wk', 'bk', 'Wv', 'bv', 'Wo', 'bo')}
    del _L0_xattn_all

    def _L0_ffn_setup():
        import jax, jax.numpy as jnp
        import numpy as np
        EPS = 1e-05

        def act_quant(x):
            scale = 127.0 / jnp.clip(jnp.max(jnp.abs(x), axis=-1, keepdims=True), EPS, None)
            xq = jnp.clip(jnp.round(x * scale), -128.0, 127.0)
            return (xq, scale)

        def weight_quant(w):
            scale = 1.0 / jnp.clip(jnp.mean(jnp.abs(w)), EPS, None)
            wq = jnp.clip(jnp.round(w * scale), -1.0, 1.0)
            return (wq, scale)

        def qlinear(x, w, b):
            xq, sx = act_quant(x)
            wq, sw = weight_quant(w)
            y = jnp.einsum('bsd,hd->bsh', xq, wq) / (sx * sw)
            return y + b

        def layernorm(x, gamma, beta):
            mu = jnp.mean(x, axis=-1, keepdims=True)
            var = jnp.mean(jnp.square(x - mu), axis=-1, keepdims=True)
            return (x - mu) * jax.lax.rsqrt(var + EPS) * gamma + beta
        key = jax.random.key(seed)
        ks = jax.random.split(key, 6)
        dim, hidden = (128, 512)
        B, S = (4, 256)
        x = jax.random.normal(ks[0], (B, S, dim), dtype=jnp.float32)
        w1 = jax.random.normal(ks[1], (hidden, dim), dtype=jnp.float32) * (1.0 / np.sqrt(dim))
        b1 = jnp.zeros((hidden,), dtype=jnp.float32)
        w2 = jax.random.normal(ks[2], (dim, hidden), dtype=jnp.float32) * (1.0 / np.sqrt(hidden))
        b2 = jnp.zeros((dim,), dtype=jnp.float32)
        gamma = jnp.ones((dim,), dtype=jnp.float32)
        beta = jnp.zeros((dim,), dtype=jnp.float32)
        return {'x': x, 'w1': w1, 'b1': b1, 'w2': w2, 'b2': b2, 'gamma': gamma, 'beta': beta}
    _L0_ffn_all = _L0_ffn_setup()
    _L0_ffn_in = {k: v for k, v in _L0_ffn_all.items() if k in ('w1', 'b1', 'w2', 'b2', 'gamma', 'beta')}
    del _L0_ffn_all

    def _L1_xattn_setup():
        import jax, jax.numpy as jnp
        import numpy as np
        H, D, C1, C2, S, M, B, W = (16, 32, 128, 64, 256, 64, 2, 4)

        def _ln(x, g, b):
            m = jnp.mean(x, -1, keepdims=True)
            v = jnp.var(x, -1, keepdims=True)
            return (x - m) * jax.lax.rsqrt(v + 1e-05) * g + b

        def _mha(x, y, wq, wk, wv, li1_w, li1_b, lnx_g, lnx_b, lny_g, lny_b, ln3_g, ln3_b, li2_w, li2_b, li3_w, li3_b, causal):
            xn = _ln(x, lnx_g, lnx_b)
            yn = _ln(y, lny_g, lny_b)
            q = jnp.einsum('bsc,hcd->bhsd', xn, wq)
            k = jnp.einsum('btc,hcd->bhtd', yn, wk)
            v = jnp.einsum('btc,hcd->bhtd', yn, wv)
            a = jax.nn.softmax(jnp.einsum('bhsd,bhtd->bhst', q, k) * D ** (-0.5), axis=-1)
            if causal:
                s, t = (a.shape[-2], a.shape[-1])
                mask = (jnp.arange(t)[None, :] > jnp.arange(s)[:, None]).astype(a.dtype)
                a = a * mask
            o = jnp.einsum('bhst,bhtd->bhsd', a, v)
            o = o.transpose(0, 2, 1, 3).reshape(x.shape[0], x.shape[1], H * D)
            x_out = x + o @ li1_w + li1_b
            h = jax.nn.gelu(_ln(x_out, ln3_g, ln3_b) @ li2_w + li2_b, approximate=False)
            return x_out + h @ li3_w + li3_b
        key = jax.random.key(seed)
        ks = iter(jax.random.split(key, 64))

        def w(shape, scale=0.02):
            return jax.random.normal(next(ks), shape, jnp.float32) * scale
        inp = {'xx': jax.random.normal(next(ks), (B, S, C1), jnp.float32), 'ee': jax.random.normal(next(ks), (B, M, C2), jnp.float32), 'ln1_g': jnp.ones(C1, jnp.float32), 'ln1_b': jnp.zeros(C1, jnp.float32), 'ln2_g': jnp.ones(C1, jnp.float32), 'ln2_b': jnp.zeros(C1, jnp.float32)}
        for pfx, cy in (('a1', C1), ('a2', C2)):
            inp[pfx + '_wq'] = w((H, C1, D))
            inp[pfx + '_wk'] = w((H, cy, D))
            inp[pfx + '_wv'] = w((H, cy, D))
            inp[pfx + '_li1_w'] = w((H * D, C1))
            inp[pfx + '_li1_b'] = jnp.zeros(C1, jnp.float32)
            inp[pfx + '_lnx_g'] = jnp.ones(C1, jnp.float32)
            inp[pfx + '_lnx_b'] = jnp.zeros(C1, jnp.float32)
            inp[pfx + '_lny_g'] = jnp.ones(cy, jnp.float32)
            inp[pfx + '_lny_b'] = jnp.zeros(cy, jnp.float32)
            inp[pfx + '_ln3_g'] = jnp.ones(C1, jnp.float32)
            inp[pfx + '_ln3_b'] = jnp.zeros(C1, jnp.float32)
            inp[pfx + '_li2_w'] = w((C1, C1 * W))
            inp[pfx + '_li2_b'] = jnp.zeros(C1 * W, jnp.float32)
            inp[pfx + '_li3_w'] = w((C1 * W, C1))
            inp[pfx + '_li3_b'] = jnp.zeros(C1, jnp.float32)
        inp['training'] = 0
        return inp
    _L1_xattn_all = _L1_xattn_setup()
    _L1_xattn_in = {k: v for k, v in _L1_xattn_all.items() if k in ('ln1_g', 'ln1_b', 'ln2_g', 'ln2_b', 'a1_wq', 'a1_wk', 'a1_wv', 'a1_li1_w', 'a1_li1_b', 'a1_lnx_g', 'a1_lnx_b', 'a1_lny_g', 'a1_lny_b', 'a1_ln3_g', 'a1_ln3_b', 'a1_li2_w', 'a1_li2_b', 'a1_li3_w', 'a1_li3_b', 'a2_wq', 'a2_wk', 'a2_wv', 'a2_li1_w', 'a2_li1_b', 'a2_lnx_g', 'a2_lnx_b', 'a2_lny_g', 'a2_lny_b', 'a2_ln3_g', 'a2_ln3_b', 'a2_li2_w', 'a2_li2_b', 'a2_li3_w', 'a2_li3_b')}
    del _L1_xattn_all

    def _L1_ffn_setup():
        import jax, jax.numpy as jnp
        import numpy as np
        B, S, D, H, E = (2, 256, 128, 16, 8)
        DH = D // H
        CAP_FACTOR = 1.2

        def _forward(embed, Wq, bq, Wk, bk, Wv, bv, We, be, Wsw, bsw, gamma, beta):
            b, s, d = embed.shape
            h, e = (Wq.shape[0], We.shape[0])
            q = jnp.einsum('bsd,hed->bhse', embed, Wq) + bq[None, :, None, :]
            k = jnp.einsum('bsd,hed->bhse', embed, Wk) + bk[None, :, None, :]
            v = jnp.einsum('bsd,hed->bhse', embed, Wv) + bv[None, :, None, :]
            att = jnp.einsum('bhse,bhte->bhst', q, k)
            tril = jnp.tril(jnp.ones((s, s), bool))
            att = jnp.where(tril, att, 0.0) / jnp.sqrt(jnp.float32(d))
            att = jax.nn.softmax(att, axis=-1)
            out = jnp.einsum('bhst,bhte->bhse', att, v)
            hiddens = out.transpose(0, 2, 1, 3).reshape(b, s, d)
            x = hiddens.reshape(-1, d)
            n = b * s
            capacity = int(CAP_FACTOR * n / e)
            logits = x @ Wsw.T + bsw
            probs = jax.nn.softmax(logits, axis=-1)
            route_probs = jnp.max(probs, axis=-1)
            routes = jnp.argmax(probs, axis=-1)
            onehot = jax.nn.one_hot(routes, e, dtype=jnp.int32)
            pos = jnp.cumsum(onehot, axis=0) - 1
            pos = jnp.take_along_axis(pos, routes[:, None], axis=1)[:, 0]
            kept = pos < capacity
            slot = jnp.where(kept, routes * capacity + pos, e * capacity)
            dispatch = jnp.zeros((e * capacity + 1, d), x.dtype).at[slot].set(x)
            expert_in = dispatch[:e * capacity].reshape(e, capacity, d)
            expert_out = jnp.einsum('ecd,efd->ecf', expert_in, We) + be[:, None, :]
            expert_flat = jnp.concatenate([expert_out.reshape(e * capacity, d), jnp.zeros((1, d), x.dtype)], 0)
            gathered = expert_flat[slot]
            y = jnp.where(kept[:, None], gathered, x)
            y = (y * route_probs[:, None]).reshape(b, s, d)
            x2 = y + embed
            mean = jnp.mean(x2, axis=-1, keepdims=True)
            var = jnp.var(x2, axis=-1, keepdims=True)
            return (x2 - mean) / jnp.sqrt(var + 1e-05) * gamma + beta
        key = jax.random.key(seed)
        ks = jax.random.split(key, 14)
        s = 0.02
        return {'embed': jax.random.normal(ks[0], (B, S, D), jnp.float32), 'Wq': jax.random.normal(ks[1], (H, DH, D), jnp.float32) * s, 'bq': jnp.zeros((H, DH), jnp.float32), 'Wk': jax.random.normal(ks[2], (H, DH, D), jnp.float32) * s, 'bk': jnp.zeros((H, DH), jnp.float32), 'Wv': jax.random.normal(ks[3], (H, DH, D), jnp.float32) * s, 'bv': jnp.zeros((H, DH), jnp.float32), 'We': jax.random.normal(ks[4], (E, D, D), jnp.float32) * s, 'be': jnp.zeros((E, D), jnp.float32), 'Wsw': jax.random.normal(ks[5], (E, D), jnp.float32) * s, 'bsw': jnp.zeros((E,), jnp.float32), 'gamma': jnp.ones((D,), jnp.float32), 'beta': jnp.zeros((D,), jnp.float32)}
    _L1_ffn_all = _L1_ffn_setup()
    _L1_ffn_in = {k: v for k, v in _L1_ffn_all.items() if k in ('Wq', 'bq', 'Wk', 'bk', 'Wv', 'bv', 'We', 'be', 'Wsw', 'bsw', 'gamma', 'beta')}
    del _L1_ffn_all

    def _L2_xattn_setup():
        import jax, jax.numpy as jnp
        import numpy as np
        B, LQ, LK = (8, 256, 256)
        QD, KD, VD = (128, 64, 64)
        key = jax.random.key(seed)
        ks = jax.random.split(key, 9)
        s = 0.02
        return {'query': jax.random.normal(ks[0], (B, LQ, QD), jnp.float32), 'key': jax.random.normal(ks[1], (B, LK, KD), jnp.float32), 'value': jax.random.normal(ks[2], (B, LK, VD), jnp.float32), 'Wq': jax.random.normal(ks[3], (QD, QD), jnp.float32) * s, 'bq': jnp.zeros((QD,), jnp.float32), 'Wk': jax.random.normal(ks[4], (KD, QD), jnp.float32) * s, 'bk': jnp.zeros((QD,), jnp.float32), 'Wv': jax.random.normal(ks[5], (VD, QD), jnp.float32) * s, 'bv': jnp.zeros((QD,), jnp.float32)}
    _L2_xattn_all = _L2_xattn_setup()
    _L2_xattn_in = {k: v for k, v in _L2_xattn_all.items() if k in ('Wq', 'bq', 'Wk', 'bk', 'Wv', 'bv')}
    del _L2_xattn_all

    def _L2_ffn_setup():
        import jax, jax.numpy as jnp
        import numpy as np
        key = jax.random.key(seed)
        ks = jax.random.split(key, 6)
        B, L, D, E = (4, 256, 128, 4)
        H = 4 * D
        x = jax.random.normal(ks[0], (B, L, D), dtype=jnp.float32)
        rW1 = jax.random.normal(ks[1], (D, 2 * D), dtype=jnp.float32) * (2.0 / D) ** 0.5
        rb1 = jnp.zeros((2 * D,), dtype=jnp.float32)
        rW2 = jax.random.normal(ks[2], (2 * D, E), dtype=jnp.float32) * (2.0 / (2 * D)) ** 0.5
        rb2 = jnp.zeros((E,), dtype=jnp.float32)
        We1 = jax.random.normal(ks[3], (E, D, H), dtype=jnp.float32) * (2.0 / D) ** 0.5
        be1 = jnp.zeros((E, H), dtype=jnp.float32)
        We2 = jax.random.normal(ks[4], (E, H, D), dtype=jnp.float32) * (2.0 / H) ** 0.5
        be2 = jnp.zeros((E, D), dtype=jnp.float32)
        return {'x': x, 'rW1': rW1, 'rb1': rb1, 'rW2': rW2, 'rb2': rb2, 'We1': We1, 'be1': be1, 'We2': We2, 'be2': be2}
    _L2_ffn_all = _L2_ffn_setup()
    _L2_ffn_in = {k: v for k, v in _L2_ffn_all.items() if k in ('rW1', 'rb1', 'rW2', 'rb2', 'We1', 'be1', 'We2', 'be2')}
    del _L2_ffn_all

    def _L3_xattn_setup():
        import jax, jax.numpy as jnp
        import numpy as np
        DIM = 128
        LATENT_DIM = 64
        NUM_HEADS = 16
        HEAD_DIM = DIM // NUM_HEADS
        SCALE = HEAD_DIM ** (-0.5)
        key = jax.random.key(seed)
        k1, k2, k3, k4, k5 = jax.random.split(key, 5)
        B, xN, zN = (2, 256, 256)
        x = jax.random.normal(k1, (B, xN, DIM), dtype=jnp.float32)
        z = jax.random.normal(k2, (B, zN, LATENT_DIM), dtype=jnp.float32)
        Wq = jax.random.normal(k3, (DIM, DIM), dtype=jnp.float32) * DIM ** (-0.5)
        Wkv = jax.random.normal(k4, (2 * DIM, LATENT_DIM), dtype=jnp.float32) * LATENT_DIM ** (-0.5)
        Wo = jax.random.normal(k5, (DIM, DIM), dtype=jnp.float32) * DIM ** (-0.5)
        return {'x': x, 'z': z, 'Wq': Wq, 'Wkv': Wkv, 'Wo': Wo}
    _L3_xattn_all = _L3_xattn_setup()
    _L3_xattn_in = {k: v for k, v in _L3_xattn_all.items() if k in ('Wq', 'Wkv', 'Wo')}
    del _L3_xattn_all

    def _L3_ffn_setup():
        import jax, jax.numpy as jnp
        import numpy as np
        D = 128
        H = 4
        DF = 512
        E = 8
        EPS = 1e-05

        def _layer_norm(x, g, b):
            mu = jnp.mean(x, axis=-1, keepdims=True)
            var = jnp.mean(jnp.square(x - mu), axis=-1, keepdims=True)
            return (x - mu) * jax.lax.rsqrt(var + EPS) * g + b

        def _mha(x, Wqkv, bqkv, Wo, bo):
            S, B, _ = x.shape
            hd = D // H
            qkv = x @ Wqkv.T + bqkv
            q, k, v = jnp.split(qkv, 3, axis=-1)
            to_heads = lambda t: t.reshape(S, B, H, hd).transpose(1, 2, 0, 3)
            q, k, v = (to_heads(q), to_heads(k), to_heads(v))
            scores = jnp.einsum('bhqd,bhkd->bhqk', q, k) * (1.0 / np.sqrt(hd))
            att = jax.nn.softmax(scores, axis=-1)
            o = jnp.einsum('bhqk,bhkd->bhqd', att, v)
            o = o.transpose(2, 0, 1, 3).reshape(S, B, D)
            return o @ Wo.T + bo

        def _moe(x, Wg, W1, b1, W2, b2):
            S, B, _ = x.shape
            xf = x.reshape(S * B, D)
            logits = xf @ Wg.T
            idx = jnp.argmax(logits, axis=-1)
            out = jnp.zeros_like(xf)
            for e in range(E):
                m = (idx == e)[:, None].astype(xf.dtype)
                h = jax.nn.relu(xf @ W1[e] + b1[e])
                out = out + m * (h @ W2[e] + b2[e])
            return out.reshape(S, B, D)
        key = jax.random.key(seed)
        ks = jax.random.split(key, 16)
        S, B = (64, 8)
        s = lambda k, shape, fan: jax.random.normal(k, shape, jnp.float32) * (1.0 / np.sqrt(fan))
        return {'x': jax.random.normal(ks[0], (S, B, D), jnp.float32), 'Wqkv': s(ks[1], (3 * D, D), D), 'bqkv': jnp.zeros((3 * D,), jnp.float32), 'Wo': s(ks[2], (D, D), D), 'bo': jnp.zeros((D,), jnp.float32), 'g1': jnp.ones((D,), jnp.float32), 'be1': jnp.zeros((D,), jnp.float32), 'g2': jnp.ones((D,), jnp.float32), 'be2': jnp.zeros((D,), jnp.float32), 'Wg': s(ks[3], (E, D), D), 'W1': s(ks[4], (E, D, DF), D), 'b1': jnp.zeros((E, DF), jnp.float32), 'W2': s(ks[5], (E, DF, D), DF), 'b2': jnp.zeros((E, D), jnp.float32)}
    _L3_ffn_all = _L3_ffn_setup()
    _L3_ffn_in = {k: v for k, v in _L3_ffn_all.items() if k in ('Wqkv', 'bqkv', 'Wo', 'bo', 'g1', 'be1', 'g2', 'be2', 'Wg', 'W1', 'b1', 'W2', 'b2')}
    del _L3_ffn_all
    return {'x': x, 'ctx_512': ctx_512, 'g_xattn': g_xattn, 'g_ffn': g_ffn, 'L0_xattn_Wq': _L0_xattn_in['Wq'], 'L0_xattn_bq': _L0_xattn_in['bq'], 'L0_xattn_Wk': _L0_xattn_in['Wk'], 'L0_xattn_bk': _L0_xattn_in['bk'], 'L0_xattn_Wv': _L0_xattn_in['Wv'], 'L0_xattn_bv': _L0_xattn_in['bv'], 'L0_xattn_Wo': _L0_xattn_in['Wo'], 'L0_xattn_bo': _L0_xattn_in['bo'], 'L0_ffn_w1': _L0_ffn_in['w1'], 'L0_ffn_b1': _L0_ffn_in['b1'], 'L0_ffn_w2': _L0_ffn_in['w2'], 'L0_ffn_b2': _L0_ffn_in['b2'], 'L0_ffn_gamma': _L0_ffn_in['gamma'], 'L0_ffn_beta': _L0_ffn_in['beta'], 'L1_xattn_ln1_g': _L1_xattn_in['ln1_g'], 'L1_xattn_ln1_b': _L1_xattn_in['ln1_b'], 'L1_xattn_ln2_g': _L1_xattn_in['ln2_g'], 'L1_xattn_ln2_b': _L1_xattn_in['ln2_b'], 'L1_xattn_a1_wq': _L1_xattn_in['a1_wq'], 'L1_xattn_a1_wk': _L1_xattn_in['a1_wk'], 'L1_xattn_a1_wv': _L1_xattn_in['a1_wv'], 'L1_xattn_a1_li1_w': _L1_xattn_in['a1_li1_w'], 'L1_xattn_a1_li1_b': _L1_xattn_in['a1_li1_b'], 'L1_xattn_a1_lnx_g': _L1_xattn_in['a1_lnx_g'], 'L1_xattn_a1_lnx_b': _L1_xattn_in['a1_lnx_b'], 'L1_xattn_a1_lny_g': _L1_xattn_in['a1_lny_g'], 'L1_xattn_a1_lny_b': _L1_xattn_in['a1_lny_b'], 'L1_xattn_a1_ln3_g': _L1_xattn_in['a1_ln3_g'], 'L1_xattn_a1_ln3_b': _L1_xattn_in['a1_ln3_b'], 'L1_xattn_a1_li2_w': _L1_xattn_in['a1_li2_w'], 'L1_xattn_a1_li2_b': _L1_xattn_in['a1_li2_b'], 'L1_xattn_a1_li3_w': _L1_xattn_in['a1_li3_w'], 'L1_xattn_a1_li3_b': _L1_xattn_in['a1_li3_b'], 'L1_xattn_a2_wq': _L1_xattn_in['a2_wq'], 'L1_xattn_a2_wk': _L1_xattn_in['a2_wk'], 'L1_xattn_a2_wv': _L1_xattn_in['a2_wv'], 'L1_xattn_a2_li1_w': _L1_xattn_in['a2_li1_w'], 'L1_xattn_a2_li1_b': _L1_xattn_in['a2_li1_b'], 'L1_xattn_a2_lnx_g': _L1_xattn_in['a2_lnx_g'], 'L1_xattn_a2_lnx_b': _L1_xattn_in['a2_lnx_b'], 'L1_xattn_a2_lny_g': _L1_xattn_in['a2_lny_g'], 'L1_xattn_a2_lny_b': _L1_xattn_in['a2_lny_b'], 'L1_xattn_a2_ln3_g': _L1_xattn_in['a2_ln3_g'], 'L1_xattn_a2_ln3_b': _L1_xattn_in['a2_ln3_b'], 'L1_xattn_a2_li2_w': _L1_xattn_in['a2_li2_w'], 'L1_xattn_a2_li2_b': _L1_xattn_in['a2_li2_b'], 'L1_xattn_a2_li3_w': _L1_xattn_in['a2_li3_w'], 'L1_xattn_a2_li3_b': _L1_xattn_in['a2_li3_b'], 'L1_ffn_Wq': _L1_ffn_in['Wq'], 'L1_ffn_bq': _L1_ffn_in['bq'], 'L1_ffn_Wk': _L1_ffn_in['Wk'], 'L1_ffn_bk': _L1_ffn_in['bk'], 'L1_ffn_Wv': _L1_ffn_in['Wv'], 'L1_ffn_bv': _L1_ffn_in['bv'], 'L1_ffn_We': _L1_ffn_in['We'], 'L1_ffn_be': _L1_ffn_in['be'], 'L1_ffn_Wsw': _L1_ffn_in['Wsw'], 'L1_ffn_bsw': _L1_ffn_in['bsw'], 'L1_ffn_gamma': _L1_ffn_in['gamma'], 'L1_ffn_beta': _L1_ffn_in['beta'], 'L2_xattn_Wq': _L2_xattn_in['Wq'], 'L2_xattn_bq': _L2_xattn_in['bq'], 'L2_xattn_Wk': _L2_xattn_in['Wk'], 'L2_xattn_bk': _L2_xattn_in['bk'], 'L2_xattn_Wv': _L2_xattn_in['Wv'], 'L2_xattn_bv': _L2_xattn_in['bv'], 'L2_ffn_rW1': _L2_ffn_in['rW1'], 'L2_ffn_rb1': _L2_ffn_in['rb1'], 'L2_ffn_rW2': _L2_ffn_in['rW2'], 'L2_ffn_rb2': _L2_ffn_in['rb2'], 'L2_ffn_We1': _L2_ffn_in['We1'], 'L2_ffn_be1': _L2_ffn_in['be1'], 'L2_ffn_We2': _L2_ffn_in['We2'], 'L2_ffn_be2': _L2_ffn_in['be2'], 'L3_xattn_Wq': _L3_xattn_in['Wq'], 'L3_xattn_Wkv': _L3_xattn_in['Wkv'], 'L3_xattn_Wo': _L3_xattn_in['Wo'], 'L3_ffn_Wqkv': _L3_ffn_in['Wqkv'], 'L3_ffn_bqkv': _L3_ffn_in['bqkv'], 'L3_ffn_Wo': _L3_ffn_in['Wo'], 'L3_ffn_bo': _L3_ffn_in['bo'], 'L3_ffn_g1': _L3_ffn_in['g1'], 'L3_ffn_be1': _L3_ffn_in['be1'], 'L3_ffn_g2': _L3_ffn_in['g2'], 'L3_ffn_be2': _L3_ffn_in['be2'], 'L3_ffn_Wg': _L3_ffn_in['Wg'], 'L3_ffn_W1': _L3_ffn_in['W1'], 'L3_ffn_b1': _L3_ffn_in['b1'], 'L3_ffn_W2': _L3_ffn_in['W2'], 'L3_ffn_b2': _L3_ffn_in['b2']}

def reference(x, ctx_512, g_xattn, g_ffn, L0_xattn_Wq, L0_xattn_bq, L0_xattn_Wk, L0_xattn_bk, L0_xattn_Wv, L0_xattn_bv, L0_xattn_Wo, L0_xattn_bo, L0_ffn_w1, L0_ffn_b1, L0_ffn_w2, L0_ffn_b2, L0_ffn_gamma, L0_ffn_beta, L1_xattn_ln1_g, L1_xattn_ln1_b, L1_xattn_ln2_g, L1_xattn_ln2_b, L1_xattn_a1_wq, L1_xattn_a1_wk, L1_xattn_a1_wv, L1_xattn_a1_li1_w, L1_xattn_a1_li1_b, L1_xattn_a1_lnx_g, L1_xattn_a1_lnx_b, L1_xattn_a1_lny_g, L1_xattn_a1_lny_b, L1_xattn_a1_ln3_g, L1_xattn_a1_ln3_b, L1_xattn_a1_li2_w, L1_xattn_a1_li2_b, L1_xattn_a1_li3_w, L1_xattn_a1_li3_b, L1_xattn_a2_wq, L1_xattn_a2_wk, L1_xattn_a2_wv, L1_xattn_a2_li1_w, L1_xattn_a2_li1_b, L1_xattn_a2_lnx_g, L1_xattn_a2_lnx_b, L1_xattn_a2_lny_g, L1_xattn_a2_lny_b, L1_xattn_a2_ln3_g, L1_xattn_a2_ln3_b, L1_xattn_a2_li2_w, L1_xattn_a2_li2_b, L1_xattn_a2_li3_w, L1_xattn_a2_li3_b, L1_ffn_Wq, L1_ffn_bq, L1_ffn_Wk, L1_ffn_bk, L1_ffn_Wv, L1_ffn_bv, L1_ffn_We, L1_ffn_be, L1_ffn_Wsw, L1_ffn_bsw, L1_ffn_gamma, L1_ffn_beta, L2_xattn_Wq, L2_xattn_bq, L2_xattn_Wk, L2_xattn_bk, L2_xattn_Wv, L2_xattn_bv, L2_ffn_rW1, L2_ffn_rb1, L2_ffn_rW2, L2_ffn_rb2, L2_ffn_We1, L2_ffn_be1, L2_ffn_We2, L2_ffn_be2, L3_xattn_Wq, L3_xattn_Wkv, L3_xattn_Wo, L3_ffn_Wqkv, L3_ffn_bqkv, L3_ffn_Wo, L3_ffn_bo, L3_ffn_g1, L3_ffn_be1, L3_ffn_g2, L3_ffn_be2, L3_ffn_Wg, L3_ffn_W1, L3_ffn_b1, L3_ffn_W2, L3_ffn_b2):
    import jax
    import jax.numpy as jnp

    def _L0_xattn_ref(q, k, v, Wq, bq, Wk, bk, Wv, bv, Wo, bo):
        import jax, jax.numpy as jnp
        import numpy as np
        HEADS = 16
        D_MODEL = 128
        IMG_MODEL = 64
        D_K = D_MODEL // HEADS
        B, LQ, _ = q.shape
        LKV = k.shape[1]
        qh = (q @ Wq + bq).reshape(B, LQ, HEADS, D_K).transpose(0, 2, 1, 3)
        kh = (k @ Wk + bk).reshape(B, LKV, HEADS, D_K).transpose(0, 2, 1, 3)
        vh = (v @ Wv + bv).reshape(B, LKV, HEADS, D_K).transpose(0, 2, 1, 3)
        scale = 1.0 / np.sqrt(D_K)
        scores = jnp.einsum('bhqd,bhkd->bhqk', qh, kh) * scale
        attn = jax.nn.softmax(scores, axis=-1)
        out = jnp.einsum('bhqk,bhkd->bhqd', attn, vh)
        concat = out.transpose(0, 2, 1, 3).reshape(B, LQ, D_MODEL)
        return concat @ Wo + bo

    def _L0_ffn_ref(x, w1, b1, w2, b2, gamma, beta):
        import jax, jax.numpy as jnp
        import numpy as np
        EPS = 1e-05

        def act_quant(x):
            scale = 127.0 / jnp.clip(jnp.max(jnp.abs(x), axis=-1, keepdims=True), EPS, None)
            xq = jnp.clip(jnp.round(x * scale), -128.0, 127.0)
            return (xq, scale)

        def weight_quant(w):
            scale = 1.0 / jnp.clip(jnp.mean(jnp.abs(w)), EPS, None)
            wq = jnp.clip(jnp.round(w * scale), -1.0, 1.0)
            return (wq, scale)

        def qlinear(x, w, b):
            xq, sx = act_quant(x)
            wq, sw = weight_quant(w)
            y = jnp.einsum('bsd,hd->bsh', xq, wq) / (sx * sw)
            return y + b

        def layernorm(x, gamma, beta):
            mu = jnp.mean(x, axis=-1, keepdims=True)
            var = jnp.mean(jnp.square(x - mu), axis=-1, keepdims=True)
            return (x - mu) * jax.lax.rsqrt(var + EPS) * gamma + beta
        h = layernorm(x, gamma, beta)
        h = qlinear(h, w1, b1)
        h = jax.nn.gelu(h, approximate=False)
        out = qlinear(h, w2, b2)
        return out

    def _L1_xattn_ref(xx, ee, ln1_g, ln1_b, ln2_g, ln2_b, a1_wq, a1_wk, a1_wv, a1_li1_w, a1_li1_b, a1_lnx_g, a1_lnx_b, a1_lny_g, a1_lny_b, a1_ln3_g, a1_ln3_b, a1_li2_w, a1_li2_b, a1_li3_w, a1_li3_b, a2_wq, a2_wk, a2_wv, a2_li1_w, a2_li1_b, a2_lnx_g, a2_lnx_b, a2_lny_g, a2_lny_b, a2_ln3_g, a2_ln3_b, a2_li2_w, a2_li2_b, a2_li3_w, a2_li3_b, training):
        import jax, jax.numpy as jnp
        import numpy as np
        H, D, C1, C2, S, M, B, W = (16, 32, 128, 64, 256, 64, 2, 4)

        def _ln(x, g, b):
            m = jnp.mean(x, -1, keepdims=True)
            v = jnp.var(x, -1, keepdims=True)
            return (x - m) * jax.lax.rsqrt(v + 1e-05) * g + b

        def _mha(x, y, wq, wk, wv, li1_w, li1_b, lnx_g, lnx_b, lny_g, lny_b, ln3_g, ln3_b, li2_w, li2_b, li3_w, li3_b, causal):
            xn = _ln(x, lnx_g, lnx_b)
            yn = _ln(y, lny_g, lny_b)
            q = jnp.einsum('bsc,hcd->bhsd', xn, wq)
            k = jnp.einsum('btc,hcd->bhtd', yn, wk)
            v = jnp.einsum('btc,hcd->bhtd', yn, wv)
            a = jax.nn.softmax(jnp.einsum('bhsd,bhtd->bhst', q, k) * D ** (-0.5), axis=-1)
            if causal:
                s, t = (a.shape[-2], a.shape[-1])
                mask = (jnp.arange(t)[None, :] > jnp.arange(s)[:, None]).astype(a.dtype)
                a = a * mask
            o = jnp.einsum('bhst,bhtd->bhsd', a, v)
            o = o.transpose(0, 2, 1, 3).reshape(x.shape[0], x.shape[1], H * D)
            x_out = x + o @ li1_w + li1_b
            h = jax.nn.gelu(_ln(x_out, ln3_g, ln3_b) @ li2_w + li2_b, approximate=False)
            return x_out + h @ li3_w + li3_b
        x = _ln(xx, ln1_g, ln1_b)
        x = x + _mha(x, x, a1_wq, a1_wk, a1_wv, a1_li1_w, a1_li1_b, a1_lnx_g, a1_lnx_b, a1_lny_g, a1_lny_b, a1_ln3_g, a1_ln3_b, a1_li2_w, a1_li2_b, a1_li3_w, a1_li3_b, causal=True)
        x = _ln(x, ln2_g, ln2_b)
        return x + _mha(x, ee, a2_wq, a2_wk, a2_wv, a2_li1_w, a2_li1_b, a2_lnx_g, a2_lnx_b, a2_lny_g, a2_lny_b, a2_ln3_g, a2_ln3_b, a2_li2_w, a2_li2_b, a2_li3_w, a2_li3_b, causal=False)

    def _L1_ffn_ref(embed, Wq, bq, Wk, bk, Wv, bv, We, be, Wsw, bsw, gamma, beta):
        import jax, jax.numpy as jnp
        import numpy as np
        B, S, D, H, E = (2, 256, 128, 16, 8)
        DH = D // H
        CAP_FACTOR = 1.2

        def _forward(embed, Wq, bq, Wk, bk, Wv, bv, We, be, Wsw, bsw, gamma, beta):
            b, s, d = embed.shape
            h, e = (Wq.shape[0], We.shape[0])
            q = jnp.einsum('bsd,hed->bhse', embed, Wq) + bq[None, :, None, :]
            k = jnp.einsum('bsd,hed->bhse', embed, Wk) + bk[None, :, None, :]
            v = jnp.einsum('bsd,hed->bhse', embed, Wv) + bv[None, :, None, :]
            att = jnp.einsum('bhse,bhte->bhst', q, k)
            tril = jnp.tril(jnp.ones((s, s), bool))
            att = jnp.where(tril, att, 0.0) / jnp.sqrt(jnp.float32(d))
            att = jax.nn.softmax(att, axis=-1)
            out = jnp.einsum('bhst,bhte->bhse', att, v)
            hiddens = out.transpose(0, 2, 1, 3).reshape(b, s, d)
            x = hiddens.reshape(-1, d)
            n = b * s
            capacity = int(CAP_FACTOR * n / e)
            logits = x @ Wsw.T + bsw
            probs = jax.nn.softmax(logits, axis=-1)
            route_probs = jnp.max(probs, axis=-1)
            routes = jnp.argmax(probs, axis=-1)
            onehot = jax.nn.one_hot(routes, e, dtype=jnp.int32)
            pos = jnp.cumsum(onehot, axis=0) - 1
            pos = jnp.take_along_axis(pos, routes[:, None], axis=1)[:, 0]
            kept = pos < capacity
            slot = jnp.where(kept, routes * capacity + pos, e * capacity)
            dispatch = jnp.zeros((e * capacity + 1, d), x.dtype).at[slot].set(x)
            expert_in = dispatch[:e * capacity].reshape(e, capacity, d)
            expert_out = jnp.einsum('ecd,efd->ecf', expert_in, We) + be[:, None, :]
            expert_flat = jnp.concatenate([expert_out.reshape(e * capacity, d), jnp.zeros((1, d), x.dtype)], 0)
            gathered = expert_flat[slot]
            y = jnp.where(kept[:, None], gathered, x)
            y = (y * route_probs[:, None]).reshape(b, s, d)
            x2 = y + embed
            mean = jnp.mean(x2, axis=-1, keepdims=True)
            var = jnp.var(x2, axis=-1, keepdims=True)
            return (x2 - mean) / jnp.sqrt(var + 1e-05) * gamma + beta
        return _forward(embed, Wq, bq, Wk, bk, Wv, bv, We, be, Wsw, bsw, gamma, beta)

    def _L2_xattn_ref(query, key, value, Wq, bq, Wk, bk, Wv, bv):
        import jax, jax.numpy as jnp
        import numpy as np
        B, LQ, LK = (8, 256, 256)
        QD, KD, VD = (128, 64, 64)
        q = jnp.einsum('bld,de->ble', query, Wq) + bq
        k = jnp.einsum('bld,de->ble', key, Wk) + bk
        v = jnp.einsum('bld,de->ble', value, Wv) + bv
        scores = jnp.einsum('bqe,bke->bqk', q, k)
        attn = jax.nn.softmax(scores, axis=-1)
        out = jnp.einsum('bqk,bke->bqe', attn, v)
        return out

    def _L2_ffn_ref(x, rW1, rb1, rW2, rb2, We1, be1, We2, be2):
        import jax, jax.numpy as jnp
        import numpy as np
        E = We1.shape[0]
        top_k = min(2, E)
        rh = jax.nn.gelu(x @ rW1 + rb1, approximate=False)
        router_logits = rh @ rW2 + rb2
        router_probs = jax.nn.softmax(router_logits, axis=-1)
        expert_weights, expert_indices = jax.lax.top_k(router_probs, top_k)
        one_hot = jax.nn.one_hot(expert_indices, E, dtype=x.dtype)
        token_mask = one_hot.sum(axis=2)
        combine_w = (one_hot * expert_weights[..., None]).sum(axis=2)
        out = jnp.zeros_like(x)
        for e in range(E):
            xi = x * token_mask[..., e:e + 1]
            h = jax.nn.gelu(xi @ We1[e] + be1[e], approximate=False)
            yo = h @ We2[e] + be2[e]
            out = out + yo * combine_w[..., e:e + 1]
        return out

    def _L3_xattn_ref(x, z, Wq, Wkv, Wo):
        import jax, jax.numpy as jnp
        import numpy as np
        DIM = 128
        LATENT_DIM = 64
        NUM_HEADS = 16
        HEAD_DIM = DIM // NUM_HEADS
        SCALE = HEAD_DIM ** (-0.5)
        B, xN, _ = x.shape
        _, zN, _ = z.shape
        Q = (x @ Wq.T).reshape(B, xN, NUM_HEADS, HEAD_DIM)
        KV = (z @ Wkv.T).reshape(B, zN, 2, NUM_HEADS, HEAD_DIM)
        K = KV[:, :, 0]
        V = KV[:, :, 1]
        attn = jnp.einsum('bqhd,bkhd->bhqk', Q, K) * SCALE
        attn = jax.nn.softmax(attn, axis=-1)
        O = jnp.einsum('bhqk,bkhd->bqhd', attn, V).reshape(B, xN, DIM)
        return O @ Wo.T

    def _L3_ffn_ref(x, Wqkv, bqkv, Wo, bo, g1, be1, g2, be2, Wg, W1, b1, W2, b2):
        import jax, jax.numpy as jnp
        import numpy as np
        D = 128
        H = 4
        DF = 512
        E = 8
        EPS = 1e-05

        def _layer_norm(x, g, b):
            mu = jnp.mean(x, axis=-1, keepdims=True)
            var = jnp.mean(jnp.square(x - mu), axis=-1, keepdims=True)
            return (x - mu) * jax.lax.rsqrt(var + EPS) * g + b

        def _mha(x, Wqkv, bqkv, Wo, bo):
            S, B, _ = x.shape
            hd = D // H
            qkv = x @ Wqkv.T + bqkv
            q, k, v = jnp.split(qkv, 3, axis=-1)
            to_heads = lambda t: t.reshape(S, B, H, hd).transpose(1, 2, 0, 3)
            q, k, v = (to_heads(q), to_heads(k), to_heads(v))
            scores = jnp.einsum('bhqd,bhkd->bhqk', q, k) * (1.0 / np.sqrt(hd))
            att = jax.nn.softmax(scores, axis=-1)
            o = jnp.einsum('bhqk,bhkd->bhqd', att, v)
            o = o.transpose(2, 0, 1, 3).reshape(S, B, D)
            return o @ Wo.T + bo

        def _moe(x, Wg, W1, b1, W2, b2):
            S, B, _ = x.shape
            xf = x.reshape(S * B, D)
            logits = xf @ Wg.T
            idx = jnp.argmax(logits, axis=-1)
            out = jnp.zeros_like(xf)
            for e in range(E):
                m = (idx == e)[:, None].astype(xf.dtype)
                h = jax.nn.relu(xf @ W1[e] + b1[e])
                out = out + m * (h @ W2[e] + b2[e])
            return out.reshape(S, B, D)
        y = _layer_norm(x + _mha(x, Wqkv, bqkv, Wo, bo), g1, be1)
        z = _layer_norm(y + _moe(y, Wg, W1, b1, W2, b2), g2, be2)
        return z
    x = x + jnp.tanh(g_xattn[0]) * _L0_xattn_ref(_layernorm(x, axis=-1), ctx_512, ctx_512, L0_xattn_Wq, L0_xattn_bq, L0_xattn_Wk, L0_xattn_bk, L0_xattn_Wv, L0_xattn_bv, L0_xattn_Wo, L0_xattn_bo)
    x = x + jnp.tanh(g_ffn[0]) * _L0_ffn_ref(_layernorm(x, axis=-1), L0_ffn_w1, L0_ffn_b1, L0_ffn_w2, L0_ffn_b2, L0_ffn_gamma, L0_ffn_beta)
    x = x + jnp.tanh(g_xattn[1]) * _L1_xattn_ref(_layernorm(x, axis=-1), ctx_512, L1_xattn_ln1_g, L1_xattn_ln1_b, L1_xattn_ln2_g, L1_xattn_ln2_b, L1_xattn_a1_wq, L1_xattn_a1_wk, L1_xattn_a1_wv, L1_xattn_a1_li1_w, L1_xattn_a1_li1_b, L1_xattn_a1_lnx_g, L1_xattn_a1_lnx_b, L1_xattn_a1_lny_g, L1_xattn_a1_lny_b, L1_xattn_a1_ln3_g, L1_xattn_a1_ln3_b, L1_xattn_a1_li2_w, L1_xattn_a1_li2_b, L1_xattn_a1_li3_w, L1_xattn_a1_li3_b, L1_xattn_a2_wq, L1_xattn_a2_wk, L1_xattn_a2_wv, L1_xattn_a2_li1_w, L1_xattn_a2_li1_b, L1_xattn_a2_lnx_g, L1_xattn_a2_lnx_b, L1_xattn_a2_lny_g, L1_xattn_a2_lny_b, L1_xattn_a2_ln3_g, L1_xattn_a2_ln3_b, L1_xattn_a2_li2_w, L1_xattn_a2_li2_b, L1_xattn_a2_li3_w, L1_xattn_a2_li3_b, 0)
    x = x + jnp.tanh(g_ffn[1]) * _L1_ffn_ref(_layernorm(x, axis=-1), L1_ffn_Wq, L1_ffn_bq, L1_ffn_Wk, L1_ffn_bk, L1_ffn_Wv, L1_ffn_bv, L1_ffn_We, L1_ffn_be, L1_ffn_Wsw, L1_ffn_bsw, L1_ffn_gamma, L1_ffn_beta)
    x = x + jnp.tanh(g_xattn[2]) * _L2_xattn_ref(_layernorm(x, axis=-1), ctx_512, ctx_512, L2_xattn_Wq, L2_xattn_bq, L2_xattn_Wk, L2_xattn_bk, L2_xattn_Wv, L2_xattn_bv)
    x = x + jnp.tanh(g_ffn[2]) * _L2_ffn_ref(_layernorm(x, axis=-1), L2_ffn_rW1, L2_ffn_rb1, L2_ffn_rW2, L2_ffn_rb2, L2_ffn_We1, L2_ffn_be1, L2_ffn_We2, L2_ffn_be2)
    x = x + jnp.tanh(g_xattn[3]) * _L3_xattn_ref(_layernorm(x, axis=-1), ctx_512, L3_xattn_Wq, L3_xattn_Wkv, L3_xattn_Wo)
    x = x + jnp.tanh(g_ffn[3]) * _L3_ffn_ref(_layernorm(x, axis=-1), L3_ffn_Wqkv, L3_ffn_bqkv, L3_ffn_Wo, L3_ffn_bo, L3_ffn_g1, L3_ffn_be1, L3_ffn_g2, L3_ffn_be2, L3_ffn_Wg, L3_ffn_W1, L3_ffn_b1, L3_ffn_W2, L3_ffn_b2)
    return x

_drawn_inputs = setup_inputs


def setup_inputs(seed=0):
    import zlib

    import numpy as np

    out = dict(_drawn_inputs(seed))
    spreads = {'L0_xattn_bq': (0.0, 0.1),
     'L0_xattn_bk': (0.0, 2.0),
     'L0_xattn_bv': (0.0, 0.1),
     'L0_xattn_bo': (0.0, 0.1),
     'L0_ffn_b1': (0.0, 0.1),
     'L0_ffn_b2': (0.0, 0.1),
     'L0_ffn_gamma': (1.0, 0.2),
     'L0_ffn_beta': (0.0, 0.1),
     'L1_xattn_ln1_g': (1.0, 0.2),
     'L1_xattn_ln1_b': (0.0, 0.1),
     'L1_xattn_ln2_g': (1.0, 0.2),
     'L1_xattn_ln2_b': (0.0, 0.1),
     'L1_xattn_a1_li1_b': (0.0, 0.1),
     'L1_xattn_a1_lnx_g': (1.0, 0.6),
     'L1_xattn_a1_lnx_b': (0.0, 0.8),
     'L1_xattn_a1_lny_g': (1.0, 0.6),
     'L1_xattn_a1_lny_b': (0.0, 0.282),
     'L1_xattn_a1_ln3_g': (1.0, 0.563),
     'L1_xattn_a1_ln3_b': (0.0, 0.433),
     'L1_xattn_a1_li2_b': (0.0, 0.1),
     'L1_xattn_a1_li3_b': (0.0, 0.1),
     'L1_xattn_a2_li1_b': (0.0, 0.1),
     'L1_xattn_a2_lnx_g': (1.0, 0.6),
     'L1_xattn_a2_lnx_b': (0.0, 0.8),
     'L1_xattn_a2_lny_g': (1.0, 0.588),
     'L1_xattn_a2_lny_b': (0.0, 0.316),
     'L1_xattn_a2_ln3_g': (1.0, 0.2),
     'L1_xattn_a2_ln3_b': (0.0, 0.317),
     'L1_xattn_a2_li2_b': (0.0, 0.1),
     'L1_xattn_a2_li3_b': (0.0, 0.1),
     'L1_ffn_bq': (0.0, 2.0),
     'L1_ffn_bk': (0.0, 2.0),
     'L1_ffn_bv': (0.0, 0.408),
     'L1_ffn_be': (0.0, 0.614),
     'L1_ffn_bsw': (0.0, 0.316),
     'L1_ffn_gamma': (1.0, 0.2),
     'L1_ffn_beta': (0.0, 0.1),
     'L2_xattn_bq': (0.0, 0.8),
     'L2_xattn_bk': (0.0, 2.0),
     'L2_xattn_bv': (0.0, 0.1),
     'L2_ffn_rb1': (0.0, 0.1),
     'L2_ffn_rb2': (0.0, 0.1),
     'L2_ffn_be1': (0.0, 0.1),
     'L2_ffn_be2': (0.0, 0.1),
     'L3_ffn_bqkv': (0.0, 0.1),
     'L3_ffn_bo': (0.0, 0.1),
     'L3_ffn_g1': (1.0, 0.2),
     'L3_ffn_be1': (0.0, 0.1),
     'L3_ffn_g2': (1.0, 0.2),
     'L3_ffn_be2': (0.0, 0.1),
     'L3_ffn_b1': (0.0, 0.438),
     'L3_ffn_b2': (0.0, 0.315)}
    factors = {'L1_xattn_a1_wq': 8.0,
     'L1_xattn_a1_wk': 8.0,
     'L1_xattn_a2_wq': 8.0,
     'L1_xattn_a2_wk': 8.0,
     'L1_ffn_Wq': 8.0,
     'L1_ffn_Wk': 8.0,
     'L1_ffn_Wv': 3.004,
     'L1_ffn_We': 8.0,
     'L1_ffn_Wsw': 8.0,
     'L2_xattn_Wq': 3.089,
     'L2_xattn_Wk': 3.061}
    for name, (base, spread) in spreads.items():
        noise = np.random.default_rng([zlib.crc32(name.encode()), seed]).standard_normal(out[name].shape)
        drawn = base * np.exp(spread * noise) if base else spread * noise
        out[name] = jnp.asarray(drawn.astype(out[name].dtype))
    for name, factor in factors.items():
        out[name] = (out[name] * factor).astype(out[name].dtype)
    return out
```

```python
from contextlib import ExitStack

import concourse.bass as bass
import numpy as np
from concourse import mybir

F32 = mybir.dt.float32
BF16 = mybir.dt.bfloat16
ALU = mybir.AluOpType
ACT = mybir.ActivationFunctionType
AX = mybir.AxisListType

B, S, D = 4, 512, 128
C, KC = 64, 77
HEADS = 16
HID = 512
NT = S // 128
SLOTS = 2
TURNS = B // SLOTS
E1, CAP = 8, int(1.2 * B * S / 8)
E2, E3 = 4, 8
EPS = 1e-5
MAGIC = 1.5 * 2.0 ** 23
BIG = 3.0e38


def const_table():
    i = np.arange(128)
    f = np.float32
    t = {}
    t["ident"] = np.eye(128, dtype=f)
    t["centre"] = (np.eye(128) - 1.0 / 128).astype(f)
    t["mean"] = np.full((128, 128), 1.0 / 128, f)
    c64 = np.zeros((128, 64), f)
    c64[:64] = np.eye(64) - 1.0 / 64
    t["centre64"] = c64
    m64 = np.zeros((128, 64), f)
    m64[:64] = 1.0 / 64
    t["mean64"] = m64
    t["ones"] = np.ones((128, 128), f)
    t["before"] = (i[:, None] < i[None, :]).astype(f)
    t["after_mask"] = (i[None, :] > i[:, None]).astype(f)
    t["tril_mask"] = (i[None, :] <= i[:, None]).astype(f)
    t["row8"] = (i[:, None] // 8 == np.arange(16)[None, :]).astype(f)
    t["row32"] = (i[:, None] // 32 == np.arange(4)[None, :]).astype(f)
    t["col8"] = np.tile(((i[None, :] // 8) % 4 == np.arange(4)[:, None]).astype(f).reshape(1, 512), (128, 1))
    t["head16"] = (i[:, None] == i[None, :] // 8).astype(f)
    sel = np.zeros((128, 9, 128), f)
    for e in range(9):
        sel[e, e] = 1.0
    t["sel"] = sel.reshape(128, 9 * 128)
    t["head32"] = (i[:, None] // 32 == i[None, :] // 32).astype(f) * f(32 ** -0.5)
    t["first"] = np.tile(np.arange(8, 0, -1, dtype=f)[None], (128, 1))
    t["beyond"] = np.tile((S - 128.0 * (np.arange(4) + 1)).astype(f)[None], (128, 1))
    t["eps"] = np.full((128, 1), EPS, f)
    return t


CONST = [(k, v.shape[1]) for k, v in const_table().items()]
GROUPS = {
    "l0": [("Wq", 128, 128), ("Wk", 64, 128), ("Wv", 64, 128), ("Wo", 128, 128), ("bq", 128, 1), ("bk", 128, 1),
           ("bv", 128, 1), ("bo", 128, 1), ("w1T", 128, 512), ("w2T", 128, 512), ("b1r", 128, 512),
           ("b2r", 128, 128), ("gammar", 128, 128), ("betar", 128, 128)],
    "l1": [("ln1_g", 128, 1), ("ln1_b", 128, 1), ("ln2_g", 128, 1), ("ln2_b", 128, 1)] + [
        (p + n, r, c) for p in ("a1_", "a2_") for n, r, c in
        [("wq", 128, 512), ("wk", 128 if p == "a1_" else 64, 512), ("wv", 128 if p == "a1_" else 64, 512),
         ("li1", 128, 512), ("li1_b", 128, 1), ("lnx_g", 128, 1), ("lnx_b", 128, 1),
         ("lny_g", 128 if p == "a1_" else 64, 1), ("lny_b", 128 if p == "a1_" else 64, 1), ("ln3_g", 128, 1),
         ("ln3_b", 128, 1), ("li2", 128, 512), ("li2_b", 128, 4), ("li3", 128, 512), ("li3_b", 128, 1)]],
    "l1f": [("Wq", 128, 128), ("Wk", 128, 128), ("Wv", 128, 128), ("bq", 128, 1), ("bk", 128, 1), ("bv", 128, 1),
            ("We", 128, E1 * 128), ("be", E1, 128), ("Wsw", 128, E1), ("bswr", 128, E1), ("gamma", 128, 1),
            ("beta", 128, 1)],
    "l2": [("Wq", 128, 128), ("Wk", 64, 128), ("Wv", 64, 128), ("bq", 128, 1), ("bk", 128, 1), ("bv", 128, 1),
           ("rW1", 128, 256), ("rb1", 128, 2), ("rW2", 128, 2 * E2), ("rb2r", 128, E2), ("be1", 128, E2 * 4),
           ("be2", 128, E2)],
    "l3": [("Wq", 128, 128), ("Wk", 64, 128), ("Wv", 64, 128), ("Wo", 128, 128), ("Wqkv", 128, 384),
           ("bqkv", 128, 3), ("Wo2", 128, 128), ("bo", 128, 1), ("g1", 128, 1), ("be1", 128, 1), ("g2", 128, 1),
           ("be2", 128, 1), ("Wg", 128, E3), ("b1", 128, E3 * 4), ("b2", 128, E3), ("gates", 128, 8)],
}


class Steps:

    def __init__(self, sem, table):
        self.sem, self.table, self.n, self.known = sem, table, 0, bool(table)

    def did(self, *name):
        self.n += 1
        if name:
            self.table[name] = self.n
        return self.sem, 1

    def last(self):
        return self.sem, self.n

    def __getitem__(self, name):
        name = name if isinstance(name, tuple) else (name,)
        return self.sem, self.table[name] if self.known else 1


def program(nc, xT, ctxT, const, packs, l2w, w1, w2, out, tables):
    ctx = ExitStack()
    with ctx:
        def sb(name, shape, dt=F32):
            return ctx.enter_context(nc.sbuf_tensor(name, shape, dt))

        def sem(name):
            return ctx.enter_context(nc.semaphore(name))

        ps = ctx.enter_context(nc.psum_tensor("ps", [128, 8, 512], F32))
        PSB = [ps[:, b, :] for b in range(8)]

        def lin(u):
            return PSB[u]

        def scb(i):
            return PSB[2 + i]

        def aux(u):
            return PSB[6 + u]

        ncst = sum(n for _, n in CONST)
        cst = sb("cst", [128, ncst])
        K, at = {}, 0
        for name, n in CONST:
            K[name] = cst[:, at:at + n]
            at += n
        W = {}
        wt = {}
        for g, items in GROUPS.items():
            wt[g] = sb("w_" + g, [128, sum(c for _, _, c in items)])
            at = 0
            W[g] = {}
            for name, rows, cols in items:
                W[g][name] = wt[g][0:rows, at:at + cols]
                at += cols
        identb = sb("identb", [128, 128], BF16)
        w1q = sb("w1q", [128, 512], BF16)
        w2q = sb("w2q", [128, 4, 128], BF16)
        gate = sb("gate", [128, 8])
        wabs = sb("wabs", [128, 4])
        xall = sb("xall", [128, B * S])
        call = sb("call", [64, B * KC])
        cnorm = sb("cnorm", [64, B * KC])
        xs = sb("xs", [128, SLOTS, S])
        xn = sb("xn", [128, SLOTS, S])
        sq = sb("sq", [128, SLOTS, S])
        rs = sb("rs", [128, SLOTS, S])
        x1 = sb("x1", [128, SLOTS, S])
        x2 = sb("x2", [128, SLOTS, S])
        cs = sb("cs", [64, SLOTS, KC])
        cn = sb("cn", [64, SLOTS, KC])
        qT = sb("qT", [128, SLOTS, 4, S])
        kt = sb("kt", [128, SLOTS, 4, KC])
        kbd = sb("kbd", [128, SLOTS, HEADS, KC])
        vx = sb("vx", [KC, SLOTS, 512])
        big = sb("big", [128, HEADS, S])
        pt = sb("pt", [128, 4, 1280])
        pp = sb("pp", [128, 2, 4, S])
        vt = sb("vt", [128, NT, 512])
        small = sb("small", [128, SLOTS, 336])
        base = sb("base", [128, E1])

        l2e = pt[:].rearrange("p a b -> p (a b)")[:, 0:2 * E2 * 512]
        hid = [big[:, 4 * u:4 * u + 4, :] for u in range(SLOTS)]
        PTX = big[0:KC, :, :]

        def sm(u, at, n):
            return small[:, u, at:at + n]

        loaded = {g: sem("loaded_" + g) for g in ["const", "x", "ctx", "w12", *GROUPS]}
        stored = sem("stored")
        l2_loaded = sem("l2_loaded")
        turn_ended = sem("turn_ended")
        turn_begins = sem("turn_begins")
        clearing = sem("clearing")
        turn_taken = sem("turn_taken")
        TENSOR = Steps(sem("tensor_steps"), tables[0])
        SCALAR = Steps(sem("scalar_steps"), tables[1])
        VECTOR = Steps(sem("vector_steps"), tables[2])
        POOL = Steps(sem("pool_steps"), tables[3])
        ALL = (TENSOR, SCALAR, VECTOR, POOL)
        block = ctx.enter_context(nc.Block())
        U = range(SLOTS)

        def end_turn(eng, steps, n):
            eng.drain().then_inc(turn_ended, 1)
            eng.wait_ge(turn_begins, n)
            eng.sem_inc(turn_taken, 1)
            if steps:
                steps.n = 0

        def pX(n):
            ring = pp[:].rearrange("p a b c -> p (a b c)")[:, 1024 * (n % 4):1024 * (n % 4) + 8 * KC]
            return ring.rearrange("p (b j k) -> p b j k", b=2, j=4)

        def PT(c, j, causal):
            at = ([0, 512, 896, 1152] if causal else [0, 128, 384, 768])[j]
            return pt[:, c, at:at + 128 * (4 - j if causal else j + 1)]

        def rows(a, u):
            return rows4(a[:, u, :])

        def rows4(a):
            return a.rearrange("p (b s) -> p b s", b=B)

        def ktile(g):
            return kraw[:, g, :]

        kraw = kbd[:].rearrange("p a b c -> p (a b c)")[:, 0:2048].rearrange("p (g s) -> p g s", g=4)

        def tq(u):
            return qT[:, u, 0, :].bitcast(BF16)[:, 0:512]

        def xq(u):
            return qT[:, u, 0, :].bitcast(BF16)[:, 512:1024]

        def tq2(u):
            return qT[:, u, 2:4, :].rearrange("p a b -> p (a b)").bitcast(BF16)

        def xq2(u):
            return pp[:, u, 0:2, :].rearrange("p a b -> p (a b)").bitcast(BF16).rearrange("p (c s) -> p c s", c=4)

        def cwT(u, e):
            return rs[0:e, u, :]

        def hot(u):
            return sm(u, 192, 64)

        def lg(u, e):
            return sm(u, 0, 64).rearrange("p (i e) -> p i e", i=4)[:, :, 0:e]

        @block.sync
        def _(sp):
            sp.dma_start(cst[:], const).then_inc(loaded["const"], 16)
            sp.dma_start(xall[:], xT).then_inc(loaded["x"], 16)
            sp.dma_start(call[:], ctxT).then_inc(loaded["ctx"], 16)
            for g in GROUPS:
                sp.dma_start(wt[g][:], packs[g]).then_inc(loaded[g], 16)
            end_turn(sp, None, 1)
            with sp.Fori(0, TURNS) as t:
                sp.wait_ge(*TENSOR["l1f", "AV", 1, 3])
                sp.dma_start(l2e, l2w).then_inc(l2_loaded, 16)
                sp.wait_ge(l2_loaded, 16)
                end_turn(sp, None, t + 2)
            sp.dma_start(big[:, 8:16, :], w1).then_inc(loaded["w12"], 16)
            sp.dma_start(pp[:].rearrange("p a b s -> p (a b) s"), w2).then_inc(loaded["w12"], 16)
            with sp.Fori(0, TURNS) as t:
                end_turn(sp, None, t + 2 + TURNS)
            sp.dma_start(out, xall[:]).then_inc(stored, 16)
            sp.wait_ge(stored, 16)

        @block.gpsimd
        def _(pool):
            def turn(n):
                pool.wait_ge(turn_ended, 4 * n)
                pool.sem_inc(clearing, 1)
                for steps in ALL:
                    pool.sem_clear(steps.sem)
                pool.sem_clear(l2_loaded)
                pool.sem_inc(turn_begins, 1)

            def masked_keys(tag, dh):
                for u in U:
                    for n in range(HEADS):
                        k, c = n // 4, n % 4
                        h = 4 * k + c if dh == 32 else 4 * c + k
                        if c == 0:
                            pool.wait_ge(*SCALAR[tag + " k", u, k if dh == 32 else 0])
                        if u:
                            pool.wait_ge(*TENSOR[tag, "S", 0, n, 3])
                        mask = K["row32"][:, c:c + 1] if dh == 32 else K["row8"][:, h:h + 1]
                        pool.tensor_scalar(big[:, h, :], ktile(k if dh == 32 else 0), mask, None, ALU.mult)\
                            .then_inc(*POOL.did(tag, "km", u, n))

            turn(1)
            with pool.Fori(0, TURNS) as t:
                masked_keys("a1", 32)
                masked_keys("l1f", 8)
                turn(t + 2)
                POOL.n = 0
            with pool.Fori(0, TURNS) as t:
                turn(t + 2 + TURNS)

        @block.tensor
        def _(pe):
            ident = K["ident"]

            def norm(tag, src, ready, dim=128):
                for u in U:
                    pe.wait_ge(*ready(u))
                    pe.matmul(lin(u), K["centre"], src(u), start=True, stop=True).then_inc(*TENSOR.did(tag, "c", u))
                for u in U:
                    pe.wait_ge(*SCALAR[tag, "sq", u])
                    pe.matmul(aux(u), K["mean"], sq[:, u, :], start=True, stop=True).then_inc(*TENSOR.did(tag, "v", u))

            def cross(tag, u, dh):
                def scores(n):
                    i, hf = n // 2, n % 2
                    if n >= 2:
                        pe.wait_ge(*VECTOR[tag, "sub", u, n - 2])
                    elif u:
                        pe.wait_ge(*VECTOR[tag, "sub", 0, 6 + n])
                    if n == 0:
                        pe.wait_ge(*VECTOR[tag, "kv", 1])
                        pe.wait_ge(*VECTOR[tag, "q", u])
                    for q in (2 * hf, 2 * hf + 1):
                        mm = pe.matmul(scb(2 * (n % 2) + q % 2)[:, 0:4 * KC],
                                       qT[:, u, q if dh == 32 else 0, 128 * i:128 * i + 128],
                                       kbd[:, u, 4 * q:4 * q + 4, :], start=True, stop=True)
                    mm.then_inc(*TENSOR.did(tag, "S", u, n))

                def turned(n):
                    for b in (0, 1):
                        if b == 0:
                            pe.wait_ge(*VECTOR[tag, "nrm", u, n])
                        if n:
                            pe.wait_ge(*SCALAR[tag, "ev", u, n - 1, b])
                        elif u:
                            pe.wait_ge(*SCALAR[tag, "ev", 0, 7, b])
                        for j in range(4):
                            mm = pe.transpose(aux(b)[0:KC, 128 * j:128 * j + 128], pX(n)[:, b, j, :], ident)
                        mm.then_inc(*TENSOR.did(tag, "T", u, n, b))

                scores(0)
                scores(1)
                for n in range(8):
                    if n < 6:
                        scores(n + 2)
                    turned(n)
                pe.wait_ge(*SCALAR[tag, "ev", u, 7, 1])
                if dh == 8:
                    for k in range(4):
                        for c in range(4):
                            mm = pe.matmul(lin(u)[32 * c:32 * c + 32, :], vx[:, u, 128 * k + 32 * c:128 * k + 32 * c + 32],
                                           PTX[:, 4 * c + k, :], start=k == 0, stop=k == 3,
                                           tile_position=(0, 32 * c), skip_group_check=True)
                    mm.then_inc(*TENSOR.did(tag, "AV", u, 0))
                else:
                    for k in range(4):
                        if k:
                            pe.wait_ge(*SCALAR[tag, "o", u, k - 1])
                        for c in range(4):
                            h = 4 * k + c
                            mm = pe.matmul(lin(u)[32 * c:32 * c + 32, :], vx[:, u, 32 * h:32 * h + 32],
                                           PTX[:, h, :], start=True, stop=True, tile_position=(0, 32 * c))
                        mm.then_inc(*TENSOR.did(tag, "AV", u, k))

            def self_attention(tag, u, dh):
                causal = dh == 8

                def scores(n):
                    k, c = n // 4, n % 4
                    h = 4 * k + c if dh == 32 else 4 * c + k
                    if n == 0:
                        pe.wait_ge(*VECTOR[tag, "q", u])
                    pe.wait_ge(*POOL[tag, "km", u, n])
                    for i in range(4):
                        if n:
                            pe.wait_ge(*SCALAR[tag, "exp", u, n - 1, i])
                        elif u:
                            pe.wait_ge(*SCALAR[tag, "exp", 0, 15, i])
                        w = 128 * (i + 1) if causal else 512
                        pe.matmul(scb(i)[:, 0:w], qT[:, u, k if dh == 32 else 0, 128 * i:128 * i + 128],
                                  big[:, h, 0:w], start=True, stop=True).then_inc(*TENSOR.did(tag, "S", u, n, i))

                def turned(n):
                    c = n % 4
                    pe.wait_ge(*VECTOR[tag, "nrm", u, n])
                    for j in range(4):
                        lo, hi = (j, 4) if causal else (0, j + 1)
                        at = 4 * n + j
                        if at >= 2:
                            m, jj = (at - 2) // 4, (at - 2) % 4
                            pe.wait_ge(*(SCALAR if jj % 2 == 0 else VECTOR)[tag, "ev", u, m, jj])
                        elif u:
                            pe.wait_ge(*(SCALAR if j % 2 == 0 else VECTOR)[tag, "ev", 0, 15, 2 + j])
                        for i in range(lo, hi):
                            mm = pe.transpose(aux(j % 2)[:, 128 * (i - lo):128 * (i - lo) + 128],
                                              pp[:, n % 2, i, 128 * j:128 * j + 128], ident)
                        mm.then_inc(*TENSOR.did(tag, "T", u, n, j))

                def values(k):
                    pe.wait_ge(*VECTOR[tag, "ev", u, 4 * k + 3, 3])
                    pe.wait_ge(*SCALAR[tag, "ev", u, 4 * k + 3, 2])
                    if dh == 32 and k:
                        pe.wait_ge(*SCALAR[tag, "o", u, k - 1])
                    first = True
                    for j in (range(4) if causal else (3, 2, 1, 0)):
                        lo, hi = (128 * j, 512) if causal else (0, 128 * (j + 1))
                        for c in range(4):
                            v = vt[:, j, 128 * k + 32 * c:128 * k + 32 * c + 32]
                            mm = pe.matmul(lin(u)[32 * c:32 * c + 32, lo:hi], v, PT(c, j, causal),
                                           start=first and (k == 0 or dh == 32),
                                           stop=j == (3 if causal else 0) and (k == 3 or dh == 32),
                                           tile_position=(0, 32 * c), skip_group_check=True)
                        first = False
                    mm.then_inc(*TENSOR.did(tag, "AV", u, k))

                scores(0)
                for n in range(16):
                    if n < 15:
                        scores(n + 1)
                    turned(n)
                    if n % 4 == 3:
                        values(n // 4)

            def linear(tag, w, src, ready, rows=None):
                for u in U:
                    for r in ready(u):
                        pe.wait_ge(*r)
                    pe.matmul(lin(u), w, src(u), start=True, stop=True).then_inc(*TENSOR.did(tag, u))

            def chunks4(tag, w, src, ready, last_reader):
                for u in U:
                    for r in ready(u):
                        pe.wait_ge(*r)
                    for c in range(4):
                        if u:
                            pe.wait_ge(*last_reader(c))
                        pe.matmul(scb(c), w[:, 128 * c:128 * c + 128], src(u), start=True, stop=True)\
                            .then_inc(*TENSOR.did(tag, u, c))

            def reduce4(tag, w, src, ready):
                for u in U:
                    for r in ready(u):
                        pe.wait_ge(*r)
                    for c in range(4):
                        mm = pe.matmul(lin(u), w[:, 128 * c:128 * c + 128], src(u)[:, c, :], start=c == 0, stop=c == 3)
                    mm.then_inc(*TENSOR.did(tag, u))

            def context_kv(tag, wk, wv, src, dh):
                for u in U:
                    if u:
                        pe.wait_ge(*VECTOR[tag, "kv", 0])
                    for g in range(4 if dh == 32 else 1):
                        pe.matmul(scb(0)[:, KC * g:KC * g + KC], wk[:, 128 * g:128 * g + 128], src[:, u, :],
                                  start=True, stop=True)
                    nv = 512 if dh == 32 else 128
                    pe.matmul(scb(1)[0:KC, 0:nv], src[:, u, :], wv[:, 0:nv], start=True, stop=True)\
                        .then_inc(*TENSOR.did(tag, "kv", u))

            def mlp(tag, w2, w3):
                chunks4(tag + " h", w2, lambda u: xn[:, u, :], lambda u: [VECTOR[tag + " in", u]],
                        lambda c: SCALAR[tag + " gelu", 0, c])
                reduce4(tag + " y", w3, lambda u: hid[u], lambda u: [SCALAR[tag + " gelu", u, 3]])

            def cw_turn(tag, e):
                for u in U:
                    pe.wait_ge(*VECTOR[tag + " cw", u])
                    for i in range(4):
                        mm = pe.transpose(aux(u)[0:e, 128 * i:128 * i + 128], sm(u, 64 + 16 * i, e), ident)
                    mm.then_inc(*TENSOR.did(tag + " cwT", u))

            def experts(tag, E, W1, W2, src):
                def up(n):
                    e, u = n // 2, n % 2
                    for c in range(4):
                        if n:
                            pe.wait_ge(*SCALAR[tag + " act", (n - 1) // 2, (n - 1) % 2, c])
                        mm = pe.matmul(scb(c), W1(e)[:, 128 * c:128 * c + 128], src(u), start=True, stop=True)
                        mm.then_inc(*TENSOR.did(tag + " up", e, u, c))
                    if e:
                        pe.wait_ge(*SCALAR[tag + " rep", e - 1, u])
                    pe.matmul(aux(u), K["sel"][0:E, 128 * e:128 * e + 128], cwT(u, E),
                              start=True, stop=True).then_inc(*TENSOR.did(tag + " rep", e, u))

                def down(n):
                    e, u = n // 2, n % 2
                    pe.wait_ge(*SCALAR[tag + " act", e, u, 3])
                    if e:
                        pe.wait_ge(*VECTOR[tag + " out", e - 1, u])
                    for c in range(4):
                        mm = pe.matmul(lin(u), W2(e)[:, 128 * c:128 * c + 128], hid[u][:, c, :], start=c == 0,
                                       stop=c == 3)
                    mm.then_inc(*TENSOR.did(tag + " down", e, u))

                for u in U:
                    pe.wait_ge(*VECTOR[tag + " cwT", u])
                up(0)
                for n in range(2 * E):
                    if n + 1 < 2 * E:
                        up(n + 1)
                    down(n)

            pe.wait_ge(loaded["const"], 16)
            for a in (0, 1):
                pe.wait_ge(*VECTOR["wabs", a])
                pe.matmul(lin(0)[:, a:a + 1], K["ones"], wabs[:, a:a + 1], start=True, stop=True)\
                    .then_inc(*TENSOR.did("wsum", a))
            pe.wait_ge(loaded["ctx"], 16)
            NC = B * KC
            pe.matmul(lin(1)[0:64, 0:NC], K["centre64"][0:64, :], call[:], start=True, stop=True)\
                .then_inc(*TENSOR.did("ctx c"))
            pe.wait_ge(*SCALAR["ctx sq"])
            pe.matmul(aux(1)[0:64, 0:NC], K["mean64"][0:64, :], sq[0:64, 0, 0:NC], start=True, stop=True)\
                .then_inc(*TENSOR.did("ctx v"))
            end_turn(pe, TENSOR, 1)
            for g in GROUPS:
                pe.wait_ge(loaded[g], 16)

            with pe.Fori(0, TURNS) as t:
                norm("l0x", lambda u: xs[:, u, :], lambda u: VECTOR["begin", u])
                linear("l0x q", W["l0"]["Wq"], lambda u: xn[:, u, :], lambda u: [VECTOR["l0x", "n", u]])
                context_kv("l0x", W["l0"]["Wk"], W["l0"]["Wv"], cs, 8)
                for u in U:
                    cross("l0x", u, 8)
                linear("l0x y", W["l0"]["Wo"], lambda u: xn[:, u, :], lambda u: [VECTOR["l0x", "o", u]])
                for u in U:
                    pe.wait_ge(*VECTOR["l0x res", u])
                    for i in range(4):
                        mm = pe.transpose(aux(u)[:, 128 * i:128 * i + 128], xs[:, u, 128 * i:128 * i + 128], ident)
                    mm.then_inc(*TENSOR.did("l0f xt", u))
                for u in U:
                    pe.wait_ge(*VECTOR["l0f q1", u])
                    auxb = aux(u).bitcast(BF16)
                    for i in range(4):
                        mm = pe.transpose(auxb[:, 128 * i:128 * i + 128], tq(u)[:, 128 * i:128 * i + 128], identb[:])
                    mm.then_inc(*TENSOR.did("l0f q1T", u))
                for u in U:
                    pe.wait_ge(*VECTOR["l0f xq", u])
                    for i in range(4):
                        if u:
                            pe.wait_ge(*VECTOR["l0f h", 0, i])
                        pe.matmul(scb(i), xq(u)[:, 128 * i:128 * i + 128], w1q[:], start=True, stop=True)\
                            .then_inc(*TENSOR.did("l0f h", u, i))
                for u in U:
                    pe.wait_ge(*VECTOR["l0f q2", u])
                    for i in range(4):
                        if u:
                            pe.wait_ge(*SCALAR["l0f xq2", 0, i])
                        sbb = scb(i).bitcast(BF16)
                        for c in range(4):
                            mm = pe.transpose(sbb[:, 128 * c:128 * c + 128],
                                              tq2(u)[:, 512 * i + 128 * c:512 * i + 128 * c + 128], identb[:])
                        mm.then_inc(*TENSOR.did("l0f q2T", u, i))
                for u in U:
                    for i in range(4):
                        pe.wait_ge(*SCALAR["l0f xq2", u, i])
                        for c in range(4):
                            mm = pe.matmul(lin(u)[:, 128 * i:128 * i + 128], xq2(u)[:, c, 128 * i:128 * i + 128],
                                           w2q[:, c, :], start=c == 0, stop=c == 3)
                        mm.then_inc(*TENSOR.did("l0f y", u, i))
                for u in U:
                    pe.wait_ge(*VECTOR["l0f yt", u])
                    for i in range(4):
                        mm = pe.transpose(aux(u)[:, 128 * i:128 * i + 128], xn[:, u, 128 * i:128 * i + 128], ident)
                    mm.then_inc(*TENSOR.did("l0f yT", u))
                norm("l1o", lambda u: xs[:, u, :], lambda u: VECTOR["l0f res", u])
                norm("l1a", lambda u: xn[:, u, :], lambda u: VECTOR["l1o", "n", u])
                norm("l1b", lambda u: x1[:, u, :], lambda u: VECTOR["l1 x1", u])
                w = W["l1"]
                chunks4("a1 q", w["a1_wq"], lambda u: xn[:, u, :], lambda u: [VECTOR["a1 in", u]],
                        lambda c: VECTOR["a1 q", 0, c])
                for u in U:
                    for c in range(4):
                        if c == 0:
                            pe.wait_ge(*VECTOR["a1 q", 1, 3])
                            if u:
                                pe.wait_ge(*SCALAR["a1", "exp", 0, 15, 3])
                        pe.matmul(scb(c), w["a1_wk"][:, 128 * c:128 * c + 128], x2[:, u, :], start=True, stop=True)\
                            .then_inc(*TENSOR.did("a1 k", u, c))
                    for j in range(4):
                        pe.wait_ge(*SCALAR["a1 k", u, j])
                        pe.matmul(scb(j), x2[:, u, 128 * j:128 * j + 128], w["a1_wv"], start=True, stop=True)\
                            .then_inc(*TENSOR.did("a1 v", u, j))
                    for j in range(4):
                        pe.wait_ge(*SCALAR["a1 v", u, j])
                    self_attention("a1", u, 32)
                reduce4("a1 li1", w["a1_li1"], lambda u: qT[:, u, :, :], lambda u: [SCALAR["a1", "o", u, 3]])
                norm("a1n3", lambda u: x2[:, u, :], lambda u: VECTOR["a1 x2", u])
                mlp("a1m", w["a1_li2"], w["a1_li3"])
                norm("l1c", lambda u: x1[:, u, :], lambda u: VECTOR["a1 x1", u])
                norm("l1d", lambda u: x1[:, u, :], lambda u: VECTOR["l1c x1", u])
                chunks4("a2 q", w["a2_wq"], lambda u: xn[:, u, :], lambda u: [VECTOR["a2 in", u]],
                        lambda c: VECTOR["a2 q", 0, c])
                pe.wait_ge(*VECTOR["a2", "q", 1])
                context_kv("a2", w["a2_wk"], w["a2_wv"], cn, 32)
                for u in U:
                    cross("a2", u, 32)
                reduce4("a2 li1", w["a2_li1"], lambda u: qT[:, u, :, :], lambda u: [SCALAR["a2", "o", u, 3]])
                norm("a2n3", lambda u: x2[:, u, :], lambda u: VECTOR["a2 x2", u])
                mlp("a2m", w["a2_li2"], w["a2_li3"])
                norm("l1f", lambda u: xs[:, u, :], lambda u: VECTOR["l1 res", u])
                w = W["l1f"]
                linear("l1f q", w["Wq"], lambda u: x1[:, u, :], lambda u: [VECTOR["l1f", "n", u]])
                for u in U:
                    if u:
                        pe.wait_ge(*SCALAR["l1f", "exp", 0, 15, 3])
                    pe.matmul(scb(0), w["Wk"], x1[:, u, :], start=True, stop=True).then_inc(*TENSOR.did("l1f k", u))
                    for j in range(4):
                        mm = pe.matmul(scb(1)[:, 128 * j:128 * j + 128], x1[:, u, 128 * j:128 * j + 128], w["Wv"],
                                       start=True, stop=True)
                    mm.then_inc(*TENSOR.did("l1f v", u))
                    pe.wait_ge(*VECTOR["l1f v", u])
                    pe.wait_ge(*SCALAR["l1f k", u, 3])
                    self_attention("l1f", u, 8)
                    pe.wait_ge(*SCALAR["l1f", "exp", u, 15, 3])
                    for i in range(3):
                        for j in range(i + 1, 4):
                            for k in range(4):
                                mm = pe.matmul(scb(0)[0:16, 128 * i:128 * i + 128], K["ones"][:, 0:16],
                                               vt[:, j, 128 * k:128 * k + 128], start=j == i + 1 and k == 0,
                                               stop=j == 3 and k == 3)
                    pe.wait_ge(*VECTOR["l1f e0", u])
                    for i in range(3):
                        mm = pe.transpose(scb(1)[0:16, 128 * i:128 * i + 128], sm(u, 128 + 16 * i, 16), ident)
                    mm.then_inc(*TENSOR.did("l1f tail", u))
                    pe.wait_ge(*VECTOR["l1f tail", u])
                    for i in range(3):
                        mm = pe.matmul(lin(u)[:, 128 * i:128 * i + 128], rs[0:16, u, 128 * i:128 * i + 128],
                                       sq[0:16, u, 128 * i:128 * i + 128], start=False, stop=i == 2,
                                       skip_group_check=True)
                    mm.then_inc(*TENSOR.did("l1f o", u))
                for u in U:
                    pe.wait_ge(*VECTOR["l1f o", u])
                    for i in range(4):
                        mm = pe.matmul(aux(u)[:, 16 * i:16 * i + E1], x2[:, u, 128 * i:128 * i + 128], w["Wsw"],
                                       start=True, stop=True)
                    mm.then_inc(*TENSOR.did("l1f logits", u))
                for u in U:
                    pe.wait_ge(*VECTOR["l1f hot", u])
                    for i in range(4):
                        for j in range(i + 1):
                            mm = pe.matmul(aux(u)[:, 16 * i:16 * i + E1], K["before"] if i == j else K["ones"],
                                           hot(u)[:, 16 * j:16 * j + E1], start=j == 0, stop=j == i)
                    for j in range(4):
                        mm = pe.matmul(aux(u)[:, 64:64 + E1], K["ones"], hot(u)[:, 16 * j:16 * j + E1],
                                       start=j == 0, stop=j == 3)
                    mm.then_inc(*TENSOR.did("l1f count", u))
                cw_turn("l1f", 9)

                def replicate(n):
                    e, u = n // 2, n % 2
                    if n >= 4:
                        pe.wait_ge(*VECTOR["l1f masked", (n - 4) // 2, u])
                    pe.matmul(scb(n % 4), K["sel"][0:9, 128 * e:128 * e + 128], cwT(u, 9), start=True, stop=True)\
                        .then_inc(*TENSOR.did("l1f rep", e, u))

                def expert(n):
                    e, u = n // 2, n % 2
                    pe.wait_ge(*VECTOR["l1f masked", e, u])
                    mm = pe.matmul(lin(u), w["We"][:, 128 * e:128 * e + 128] if e < E1 else ident,
                                   hid[u][:, e % 4, :], start=False, stop=e == E1)
                    mm.then_inc(*TENSOR.did("l1f expert", e, u))

                for u in U:
                    pe.wait_ge(*VECTOR["l1f cwT", u])
                    pe.matmul(lin(u), w["be"][0:E1, :], cwT(u, 8), start=True, stop=False)
                replicate(0)
                replicate(1)
                for n in range(18):
                    if n + 2 < 18:
                        replicate(n + 2)
                    expert(n)
                norm("l1g", lambda u: x2[:, u, :], lambda u: VECTOR["l1f x2", u])
                norm("l2x", lambda u: xs[:, u, :], lambda u: VECTOR["l1f res", u])
                w = W["l2"]
                linear("l2x q", w["Wq"], lambda u: xn[:, u, :], lambda u: [VECTOR["l2x", "n", u]])
                context_kv("l2x", w["Wk"], w["Wv"], cs, 8)
                for u in U:
                    pe.wait_ge(*VECTOR["l2x q", u])
                    pe.wait_ge(*VECTOR["l2x", "kv", 1])
                    for i in range(4):
                        mm = pe.matmul(scb(u)[:, KC * i:KC * i + KC], qT[:, u, 0, 128 * i:128 * i + 128],
                                       kt[:, u, 0, :], start=True, stop=True)
                    mm.then_inc(*TENSOR.did("l2x S", u))
                for u in U:
                    pe.wait_ge(*VECTOR["l2x nrm", u])
                    for i in range(4):
                        mm = pe.transpose(aux(u)[0:KC, 128 * i:128 * i + 128], pX(u)[:, 0, i, :], ident)
                    mm.then_inc(*TENSOR.did("l2x T", u))
                for u in U:
                    pe.wait_ge(*SCALAR["l2x ev", u])
                    pe.matmul(lin(u), vx[:, u, 0:128], sq[0:KC, u, :], start=True, stop=True)\
                        .then_inc(*TENSOR.did("l2x y", u))
                norm("l2f", lambda u: xs[:, u, :], lambda u: VECTOR["l2x res", u])
                for u in U:
                    pe.wait_ge(*VECTOR["l2f", "n", u])
                    for c in range(2):
                        mm = pe.matmul(scb(2 * u + c), w["rW1"][:, 128 * c:128 * c + 128], xn[:, u, :], start=True,
                                       stop=True)
                    mm.then_inc(*TENSOR.did("l2f r", u))
                for u in U:
                    pe.wait_ge(*SCALAR["l2f r", u])
                    for i in range(4):
                        for c in range(2):
                            mm = pe.matmul(aux(u)[:, 16 * i:16 * i + E2], hid[u][:, c, 128 * i:128 * i + 128],
                                           w["rW2"][:, E2 * c:E2 * c + E2], start=c == 0, stop=c == 1)
                    mm.then_inc(*TENSOR.did("l2f logits", u))
                cw_turn("l2f", E2)
                pe.wait_ge(l2_loaded, 16)
                experts("l2f", E2, lambda e: l2e[:, 512 * e:512 * e + 512],
                        lambda e: l2e[:, 512 * (E2 + e):512 * (E2 + e) + 512], lambda u: xn[:, u, :])
                norm("l3x", lambda u: xs[:, u, :], lambda u: VECTOR["l2f res", u])
                w = W["l3"]
                linear("l3x q", w["Wq"], lambda u: xn[:, u, :], lambda u: [VECTOR["l3x", "n", u]])
                context_kv("l3x", w["Wk"], w["Wv"], cs, 8)
                for u in U:
                    cross("l3x", u, 8)
                linear("l3x y", w["Wo"], lambda u: xn[:, u, :], lambda u: [VECTOR["l3x", "o", u]])
                end_turn(pe, TENSOR, t + 2)

            w = W["l3"]
            with pe.Fori(0, TURNS) as t:
                norm("l3f", lambda u: xs[:, u, :], lambda u: VECTOR["begin3", u])
                for u in U:
                    pe.wait_ge(*VECTOR["l3f", "n", u])
                    for c in range(3):
                        if u:
                            pe.wait_ge(*VECTOR["l3f qkv", 0, c])
                        pe.matmul(scb(c), w["Wqkv"][:, 128 * c:128 * c + 128], x1[:, u, :], start=True, stop=True)\
                            .then_inc(*TENSOR.did("l3f qkv", u, c))
                for i in range(4):
                    for u in U:
                        pe.wait_ge(*VECTOR["l3f prod", u, i])
                        pe.matmul(aux(u), K["head32"], sq[:, u, :], start=True, stop=True)\
                            .then_inc(*TENSOR.did("l3f S", u, i))
                linear("l3f y", w["Wo2"], lambda u: xn[:, u, :], lambda u: [VECTOR["l3f o", u, 3]])
                norm("l3g", lambda u: x2[:, u, :], lambda u: VECTOR["l3f x2", u])
                for u in U:
                    pe.wait_ge(*VECTOR["l3g aff", u])
                    for i in range(4):
                        mm = pe.matmul(aux(u)[:, 16 * i:16 * i + E3], x1[:, u, 128 * i:128 * i + 128], w["Wg"],
                                       start=True, stop=True)
                    mm.then_inc(*TENSOR.did("l3f logits", u))
                cw_turn("l3f", E3)
                pe.wait_ge(loaded["w12"], 32)
                experts("l3f", E3, lambda e: big[:, 8 + e, :], lambda e: pp[:, e // 4, e % 4, :],
                        lambda u: x1[:, u, :])
                norm("l3h", lambda u: x2[:, u, :], lambda u: VECTOR["l3f z", u])
                end_turn(pe, TENSOR, t + 2 + TURNS)

        @block.scalar
        def _(act):
            A = act.activation
            eps = K["eps"]

            def exp_set():
                act.preload_act_table_set("natural_log_exp_and_others")

            def gelu_set():
                act.preload_act_table_set("gelu_and_others")

            def norm(tag):
                for u in U:
                    act.wait_ge(*TENSOR[tag, "c", u])
                    A(sq[:, u, :], lin(u), ACT.Square).then_inc(*SCALAR.did(tag, "sq", u))
                for u in U:
                    act.wait_ge(*TENSOR[tag, "v", u])
                    A(rs[:, u, :], aux(u), ACT.Ln, bias=eps).then_inc(*SCALAR.did())
                    act.wait_ge(*SCALAR.last())
                    A(rs[:, u, :], rs[:, u, :], ACT.Exp, scale=-0.5).then_inc(*SCALAR.did(tag, "rs", u))

            def cross(tag, u, dh):
                def exp(n):
                    act.wait_ge(*VECTOR[tag, "sub", u, n])
                    A(pX(n), pX(n), ACT.Exp).then_inc(*SCALAR.did(tag, "exp", u, n))

                def out(n):
                    i, hf = n // 2, n % 2
                    for b in (0, 1):
                        act.wait_ge(*TENSOR[tag, "T", u, n, b])
                        if u and n == 0 and b == 0:
                            act.wait_ge(*TENSOR[tag, "AV", 0, 0 if dh == 8 else 3])
                        h = 8 * hf + 4 * b
                        A(PTX[:, h:h + 4, 128 * i:128 * i + 128], aux(b)[0:KC, :].rearrange("p (h s) -> p h s", h=4),
                          ACT.Identity).then_inc(*SCALAR.did(tag, "ev", u, n, b))

                exp(0)
                for n in range(8):
                    if n < 7:
                        exp(n + 1)
                    out(n)
                if dh == 32:
                    for k in range(4):
                        act.wait_ge(*TENSOR[tag, "AV", u, k])
                        A(qT[:, u, k, :], lin(u), ACT.Identity).then_inc(*SCALAR.did(tag, "o", u, k))

            def self_attention(tag, u, dh):
                causal = dh == 8

                def exps(n):
                    for i in range(4):
                        w = 128 * (i + 1) if causal else 512
                        act.wait_ge(*VECTOR[tag, "mx", u, n, i])
                        if n >= 2 and i == 0:
                            act.wait_ge(*TENSOR[tag, "T", u, n - 2, 3])
                        elif u and n < 2 and i == 0:
                            act.wait_ge(*TENSOR[tag, "T", 0, 14 + n, 3])
                        A(pp[:, n % 2, i, 0:w], scb(i)[:, 0:w], ACT.Exp, bias=sm(0, 300 + 4 * (n % 2) + i, 1),
                          accum_out=sm(0, 308 + 4 * (n % 2) + i, 1)).then_inc(*SCALAR.did(tag, "exp", u, n, i))
                    if causal:
                        A(sm(0, 316 + 4 * (n % 2), 4), sm(0, 300 + 4 * (n % 2), 4), ACT.Exp)\
                            .then_inc(*SCALAR.did(tag, "e0", u, n))

                def out(n):
                    c = n % 4
                    for j in (0, 2):
                        if n % 4 == 0 and j == 0 and n:
                            act.wait_ge(*TENSOR[tag, "AV", u, n // 4 - 1])
                        act.wait_ge(*TENSOR[tag, "T", u, n, j])
                        w = 128 * (4 - j if causal else j + 1)
                        A(PT(c, j, causal), aux(j % 2)[:, 0:w], ACT.Identity).then_inc(*SCALAR.did(tag, "ev", u, n, j))
                    if n % 4 == 3 and dh == 32:
                        act.wait_ge(*TENSOR[tag, "AV", u, n // 4])
                        A(qT[:, u, n // 4, :], lin(u), ACT.Identity).then_inc(*SCALAR.did(tag, "o", u, n // 4))

                exps(0)
                for n in range(16):
                    if n < 15:
                        exps(n + 1)
                    out(n)

            def mlp(tag, b2):
                gelu_set()
                for u in U:
                    for c in range(4):
                        act.wait_ge(*TENSOR[tag + " h", u, c])
                        A(hid[u][:, c, :], scb(c), ACT.Gelu, bias=b2[:, c:c + 1])\
                            .then_inc(*SCALAR.did(tag + " gelu", u, c))
                exp_set()

            def experts(tag, E, b1, func):
                for n in range(2 * E):
                    e, u = n // 2, n % 2
                    if n >= 2:
                        act.wait_ge(*TENSOR[tag + " down", e - 1, u])
                    for c in range(4):
                        act.wait_ge(*TENSOR[tag + " up", e, u, c])
                        A(hid[u][:, c, :], scb(c), func, bias=b1[:, 4 * e + c:4 * e + c + 1])\
                            .then_inc(*SCALAR.did(tag + " act", e, u, c))
                    act.wait_ge(*TENSOR[tag + " rep", e, u])
                    if e:
                        act.wait_ge(*VECTOR[tag + " out", e - 1, u])
                    A(sq[:, u, :], aux(u), ACT.Identity).then_inc(*SCALAR.did(tag + " rep", e, u))

            def token_rstd(tag):
                for u in U:
                    act.wait_ge(*VECTOR[tag, "st", u])
                    A(sm(u, 44, 4), sm(u, 32, 8).rearrange("p (a b) -> p a b", b=2)[:, :, 1], ACT.Ln, bias=eps)\
                        .then_inc(*SCALAR.did())
                    act.wait_ge(*SCALAR.last())
                    A(sm(u, 44, 4), sm(u, 44, 4), ACT.Exp, scale=-0.5).then_inc(*SCALAR.did(tag, "r", u))

            act.wait_ge(loaded["const"], 16)
            for g in GROUPS:
                act.wait_ge(loaded[g], 16)
            A(gate[:], W["l3"]["gates"], ACT.Tanh).then_inc(*SCALAR.did("gates"))
            NC = B * KC
            act.wait_ge(*TENSOR["ctx c"])
            A(sq[0:64, 0, 0:NC], lin(1)[0:64, 0:NC], ACT.Square).then_inc(*SCALAR.did("ctx sq"))
            act.wait_ge(*TENSOR["ctx v"])
            A(rs[0:64, 0, 0:NC], aux(1)[0:64, 0:NC], ACT.Ln, bias=eps[0:64, :]).then_inc(*SCALAR.did())
            act.wait_ge(*SCALAR.last())
            A(rs[0:64, 0, 0:NC], rs[0:64, 0, 0:NC], ACT.Exp, scale=-0.5).then_inc(*SCALAR.did("ctx rs"))
            end_turn(act, SCALAR, 1)

            with act.Fori(0, TURNS) as t:
                exp_set()
                norm("l0x")
                for u in U:
                    cross("l0x", u, 8)
                token_rstd("l0f a")
                token_rstd("l0f b")
                gelu_set()
                for u in U:
                    act.wait_ge(*VECTOR["l0f h", u, 3])
                    A(hid[u], hid[u], ACT.Gelu).then_inc(*SCALAR.did("l0f gelu", u))
                exp_set()
                for u in U:
                    for i in range(4):
                        act.wait_ge(*TENSOR["l0f q2T", u, i])
                        A(xq2(u)[:, :, 128 * i:128 * i + 128],
                          scb(i).bitcast(BF16)[:, 0:512].rearrange("p (c s) -> p c s", c=4), ACT.Identity)\
                            .then_inc(*SCALAR.did("l0f xq2", u, i))
                norm("l1o")
                norm("l1a")
                norm("l1b")
                for u in U:
                    for c in range(4):
                        act.wait_ge(*TENSOR["a1 k", u, c])
                        if c == 0 and u:
                            act.wait_ge(*TENSOR["a1", "AV", 0, 3])
                        if True:
                            A(ktile(c), scb(c), ACT.Identity).then_inc(*SCALAR.did("a1 k", u, c))
                    for j in range(4):
                        act.wait_ge(*TENSOR["a1 v", u, j])
                        A(vt[:, j, :], scb(j), ACT.Identity).then_inc(*SCALAR.did("a1 v", u, j))
                    self_attention("a1", u, 32)
                norm("a1n3")
                mlp("a1m", W["l1"]["a1_li2_b"])
                norm("l1c")
                norm("l1d")
                for u in U:
                    cross("a2", u, 32)
                norm("a2n3")
                mlp("a2m", W["l1"]["a2_li2_b"])
                norm("l1f")
                for u in U:
                    act.wait_ge(*TENSOR["l1f k", u])
                    if u:
                        act.wait_ge(*TENSOR["l1f", "AV", 0, 3])
                    for c in range(4):
                        if c == 0:
                            A(ktile(0), scb(0), ACT.Identity, bias=W["l1f"]["bk"])\
                                .then_inc(*SCALAR.did("l1f k", u, 0))
                    SCALAR.table["l1f k", u, 3] = SCALAR.table["l1f k", u, 0]
                    self_attention("l1f", u, 8)
                for u in U:
                    act.wait_ge(*VECTOR["l1f sub", u])
                    A(lg(u, E1), lg(u, E1), ACT.Exp).then_inc(*SCALAR.did("l1f e", u))
                norm("l1g")
                norm("l2x")
                for u in U:
                    act.wait_ge(*VECTOR["l2x sub", u])
                    A(pX(u)[:, 0], pX(u)[:, 0], ACT.Exp).then_inc(*SCALAR.did("l2x exp", u))
                for u in U:
                    act.wait_ge(*TENSOR["l2x T", u])
                    A(sq[0:KC, u, :], aux(u)[0:KC, :], ACT.Identity).then_inc(*SCALAR.did("l2x ev", u))
                norm("l2f")
                gelu_set()
                for u in U:
                    act.wait_ge(*TENSOR["l2f r", u])
                    for c in range(2):
                        ins = A(hid[u][:, c, :], scb(2 * u + c), ACT.Gelu, bias=W["l2"]["rb1"][:, c:c + 1])
                    ins.then_inc(*SCALAR.did("l2f r", u))
                exp_set()
                for u in U:
                    act.wait_ge(*VECTOR["l2f sub", u])
                    A(lg(u, E2), lg(u, E2), ACT.Exp).then_inc(*SCALAR.did("l2f e", u))
                gelu_set()
                experts("l2f", E2, W["l2"]["be1"], ACT.Gelu)
                exp_set()
                norm("l3x")
                for u in U:
                    cross("l3x", u, 8)
                end_turn(act, SCALAR, t + 2)

            with act.Fori(0, TURNS) as t:
                exp_set()
                norm("l3f")
                for i in range(4):
                    for u in U:
                        act.wait_ge(*VECTOR["l3f sub", u, i])
                        A(rs[:, u, :], rs[:, u, :], ACT.Exp).then_inc(*SCALAR.did("l3f exp", u, i))
                norm("l3g")
                experts("l3f", E3, W["l3"]["b1"], ACT.Relu)
                norm("l3h")
                end_turn(act, SCALAR, t + 2 + TURNS)

        @block.vector
        def _(v):
            def chain(ins):
                ins.then_inc(*VECTOR.did())
                v.wait_ge(*VECTOR.last())

            def norm(tag, dst):
                for u in U:
                    v.wait_ge(*SCALAR[tag, "rs", u])
                    v.tensor_tensor(dst(u), lin(u), rs[:, u, :], ALU.mult).then_inc(*VECTOR.did(tag, "n", u))

            def affine(name, dst, src, g, b):
                for u in U:
                    v.wait_ge(*VECTOR.last())
                    v.tensor_scalar(dst(u), src(u), g, b, ALU.mult, ALU.add).then_inc(*VECTOR.did(name, u))

            def residual(tag, u, y, g, bias=None):
                if bias is not None:
                    chain(v.tensor_scalar(xn[:, u, :], y, bias, None, ALU.add))
                    y = xn[:, u, :]
                v.scalar_tensor_tensor(xs[:, u, :], y, gate[:, g:g + 1], xs[:, u, :], ALU.mult, ALU.add)\
                    .then_inc(*VECTOR.did(tag, u))

            def context_kv(tag, bk, dh):
                for u in U:
                    v.wait_ge(*TENSOR[tag, "kv", u])
                    g = 4 if dh == 32 else 1
                    kv = kt[:, u, 0:g, :]
                    src = scb(0)[:, 0:KC * g].rearrange("p (g k) -> p g k", g=g)
                    if bk is None:
                        chain(v.tensor_copy(kv, src))
                    else:
                        chain(v.tensor_scalar(kv, src, bk, None, ALU.add))
                    if dh == 32:
                        v.tensor_copy(vx[:, u, :], scb(1)[0:KC, :])
                        for g in range(4):
                            last = v.tensor_tensor(kbd[:, u, 4 * g:4 * g + 4, :],
                                                   kt[:, u, g:g + 1, :].to_broadcast([128, 4, KC]),
                                                   K["row32"].unsqueeze(2).to_broadcast([128, 4, KC]), ALU.mult)
                    elif tag == "l2x":
                        last = v.tensor_copy(vx[:, u, 0:128], scb(1)[0:KC, 0:128])
                    else:
                        v.tensor_tensor(vx[:, u, :].rearrange("p (k f) -> p k f", k=4),
                                        scb(1)[0:KC, 0:128].unsqueeze(1).to_broadcast([KC, 4, 128]),
                                        K["col8"][0:KC, :].rearrange("p (k f) -> p k f", k=4), ALU.mult)
                        last = v.tensor_tensor(kbd[:, u, :, :], kt[:, u, 0:1, :].to_broadcast([128, HEADS, KC]),
                                               K["row8"].unsqueeze(2).to_broadcast([128, HEADS, KC]), ALU.mult)
                    last.then_inc(*VECTOR.did(tag, "kv", u))

            def softmax_sub(S, P, mx, n):
                chain(v.tensor_reduce(mx, S, AX.X, ALU.max))
                return v.tensor_tensor(P, S, mx.unsqueeze(n).to_broadcast(list(P.shape)), ALU.subtract)

            def cross(tag, u, dh, bv):
                def sub(n):
                    v.wait_ge(*TENSOR[tag, "S", u, n])
                    if n >= 4:
                        v.wait_ge(*TENSOR[tag, "T", u, n - 4, 1])
                    elif u:
                        v.wait_ge(*TENSOR[tag, "T", 0, 4 + n, 1])
                    b = 2 + 2 * (n % 2)
                    mx = sm(0, 300 + 8 * (n % 2), 8).rearrange("p (b j) -> p b j", b=2)
                    src = ps[:, b:b + 2, 0:4 * KC].rearrange("p b (j k) -> p b j k", j=4)
                    softmax_sub(src, pX(n), mx, 3).then_inc(*VECTOR.did(tag, "sub", u, n))

                def nrm(n):
                    v.wait_ge(*SCALAR[tag, "exp", u, n])
                    P = pX(n).rearrange("p b j k -> p (b j) k")
                    s = sm(0, 320 + 8 * (n % 2), 8)
                    chain(v.tensor_reduce(s, P, AX.X, ALU.add))
                    chain(v.reciprocal(s, s))
                    v.tensor_tensor(P, P, s.unsqueeze(2).to_broadcast([128, 8, KC]), ALU.mult)\
                        .then_inc(*VECTOR.did(tag, "nrm", u, n))

                sub(0)
                for n in range(8):
                    if n < 7:
                        sub(n + 1)
                    nrm(n)
                if dh == 8:
                    v.wait_ge(*TENSOR[tag, "AV", u, 0])
                    if bv is None:
                        v.tensor_copy(xn[:, u, :], lin(u)).then_inc(*VECTOR.did(tag, "o", u))
                    else:
                        v.tensor_scalar(xn[:, u, :], lin(u), bv, None, ALU.add).then_inc(*VECTOR.did(tag, "o", u))

            def self_attention(tag, u, dh):
                causal = dh == 8

                def maxima(n):
                    for i in range(4):
                        w = 128 * (i + 1) if causal else 512
                        v.wait_ge(*TENSOR[tag, "S", u, n, i])
                        nm = sm(0, 300 + 4 * (n % 2) + i, 1)
                        if causal:
                            d = scb(i)[:, 128 * i:128 * i + 128]
                            chain(v.tensor_tensor(d, d, K["tril_mask"], ALU.mult))
                        if causal and i < 3:
                            chain(v.tensor_reduce(nm, scb(i)[:, 0:w], AX.X, ALU.max))
                            v.tensor_scalar(nm, nm, 0.0, -1.0, ALU.max, ALU.mult)\
                                .then_inc(*VECTOR.did(tag, "mx", u, n, i))
                        else:
                            v.tensor_reduce(nm, scb(i)[:, 0:w], AX.X, ALU.max, negate=True)\
                                .then_inc(*VECTOR.did(tag, "mx", u, n, i))

                def nrm(n):
                    k, c = n // 4, n % 4
                    h = 4 * k + c if dh == 32 else 4 * c + k
                    den = sm(0, 308 + 4 * (n % 2), 4)
                    inv = sm(0, 324 + 4 * (n % 2), 4)
                    v.wait_ge(*SCALAR[tag, "exp", u, n, 3])
                    if causal:
                        e0 = sm(0, 316 + 4 * (n % 2), 4)
                        v.wait_ge(*SCALAR[tag, "e0", u, n])
                        chain(v.tensor_tensor(inv, e0, K["beyond"], ALU.mult))
                        chain(v.tensor_tensor(den, den, inv, ALU.add))
                    chain(v.reciprocal(inv, den))
                    if causal:
                        v.tensor_tensor(sm(u, 128, 64).rearrange("p (i h) -> p i h", i=4)[:, :, h], e0, inv, ALU.mult)
                    for i in range(4):
                        P = pp[:, n % 2, i, :]
                        r = inv[:, i:i + 1]
                        if causal:
                            last = v.tensor_scalar(P[:, 0:128 * (i + 1)], P[:, 0:128 * (i + 1)], r, None, ALU.mult)
                        else:
                            last = v.scalar_tensor_tensor(P[:, 128 * i:128 * i + 128], P[:, 128 * i:128 * i + 128], r,
                                                          K["after_mask"], ALU.mult, ALU.mult)
                            if i < 3:
                                last = v.tensor_scalar(P[:, 128 * (i + 1):], P[:, 128 * (i + 1):], r, None, ALU.mult)
                    last.then_inc(*VECTOR.did(tag, "nrm", u, n))

                def out(n):
                    c = n % 4
                    for j in (1, 3):
                        if n % 4 == 0 and j == 1 and n:
                            v.wait_ge(*TENSOR[tag, "AV", u, n // 4 - 1])
                        v.wait_ge(*TENSOR[tag, "T", u, n, j])
                        w = 128 * (4 - j if causal else j + 1)
                        v.tensor_copy(PT(c, j, causal), aux(j % 2)[:, 0:w]).then_inc(*VECTOR.did(tag, "ev", u, n, j))

                maxima(0)
                for n in range(16):
                    nrm(n)
                    if n < 15:
                        maxima(n + 1)
                    out(n)

            def pick_first(hotv, score, mxcol, E):
                first = K["first"][:, 0:E].unsqueeze(1).to_broadcast([128, 4, E])
                m = mxcol.unsqueeze(2).to_broadcast([128, 4, E])
                chain(v.tensor_reduce(mxcol, score, AX.X, ALU.max))
                chain(v.tensor_tensor(hotv, score, m, ALU.is_equal))
                chain(v.tensor_tensor(hotv, hotv, first, ALU.mult))
                chain(v.tensor_reduce(mxcol, hotv, AX.X, ALU.max))
                return v.tensor_tensor(hotv, hotv, m, ALU.is_equal)

            def view(u, at, E):
                return sm(u, at, 64).rearrange("p (i e) -> p i e", i=4)[:, :, 0:E]

            def bc(a, E):
                return a.unsqueeze(2).to_broadcast([128, 4, E])

            def cw_turned(tag, e):
                for u in U:
                    v.wait_ge(*TENSOR[tag + " cwT", u])
                    v.tensor_copy(cwT(u, e), aux(u)[0:e, :]).then_inc(*VECTOR.did(tag + " cwT", u))

            def experts(tag, E, b2, acc):
                for n in range(2 * E):
                    e, u = n // 2, n % 2
                    v.wait_ge(*TENSOR[tag + " down", e, u])
                    v.wait_ge(*SCALAR[tag + " rep", e, u])
                    a = acc(u)
                    if e == 0:
                        v.scalar_tensor_tensor(a, lin(u), b2[:, 0:1], sq[:, u, :], ALU.add, ALU.mult)\
                            .then_inc(*VECTOR.did(tag + " out", e, u))
                    else:
                        t = kbd[:, u].rearrange("p h k -> p (h k)")[:, 0:S]
                        chain(v.scalar_tensor_tensor(t, lin(u), b2[:, e:e + 1], sq[:, u, :], ALU.add, ALU.mult))
                        v.tensor_tensor(a, a, t, ALU.add).then_inc(*VECTOR.did(tag + " out", e, u))

            def token_norm(tag, src):
                for u in U:
                    for i in range(4):
                        ins = v.bn_stats(sm(u, 6 * i, 6), src(u)[:, 128 * i:128 * i + 128])
                    chain(ins)
                    for i in range(4):
                        last = v.bn_aggr(sm(u, 32 + 2 * i, 2), sm(u, 6 * i, 6))
                    last.then_inc(*VECTOR.did(tag, "st", u))
                for u in U:
                    v.wait_ge(*SCALAR[tag, "r", u])
                    for i in range(4):
                        last = v.tensor_scalar(xn[:, u, 128 * i:128 * i + 128], src(u)[:, 128 * i:128 * i + 128],
                                               sm(u, 32 + 2 * i, 1), sm(u, 44 + i, 1), ALU.subtract, ALU.mult)
                    last.then_inc(*VECTOR.did(tag, "n", u))

            def quantise(u, src, dst, mw, at):
                am, inv = sm(u, at, 4), sm(u, at + 4, 4)
                chain(v.tensor_reduce(am, src, AX.X, ALU.max, apply_absolute_value=True))
                chain(v.tensor_scalar(am, am, EPS, None, ALU.max))
                chain(v.reciprocal(inv, am))
                v.tensor_scalar(inv, inv, 127.0, None, ALU.mult).then_inc(*VECTOR.did())
                v.tensor_scalar(am, am, mw, 1.0 / 127.0, ALU.mult, ALU.mult).then_inc(*VECTOR.did())
                v.wait_ge(*VECTOR.last())
                for i in range(4):
                    last = v.tensor_scalar(src[:, i, :], src[:, i, :], inv[:, i:i + 1], 127.0, ALU.mult, ALU.min)
                chain(last)
                chain(v.tensor_scalar(src, src, -128.0, MAGIC, ALU.max, ALU.add))
                return v.tensor_scalar(dst, src, MAGIC, None, ALU.subtract)

            v.wait_ge(loaded["const"], 16)
            v.tensor_copy(identb[:], K["ident"])
            v.wait_ge(loaded["l0"], 16)
            for a, w in enumerate((W["l0"]["w1T"], W["l0"]["w2T"])):
                v.tensor_reduce(wabs[:, a:a + 1], w, AX.X, ALU.add, apply_absolute_value=True)\
                    .then_inc(*VECTOR.did("wabs", a))
            v.wait_ge(*TENSOR["wsum", 1])
            chain(v.tensor_scalar(wabs[:, 0:2], lin(0)[:, 0:2], 1.0 / (D * HID), EPS, ALU.mult, ALU.max))
            chain(v.reciprocal(wabs[:, 2:4], wabs[:, 0:2]))
            for a, (w, wq) in enumerate(((W["l0"]["w1T"], w1q[:]), (W["l0"]["w2T"], w2q[:].rearrange("p c f -> p (c f)")))):
                chain(v.tensor_scalar(w, w, wabs[:, 2 + a:3 + a], 1.0, ALU.mult, ALU.min))
                chain(v.tensor_scalar(w, w, -1.0, MAGIC, ALU.max, ALU.add))
                chain(v.tensor_scalar(wq, w, MAGIC, None, ALU.subtract))
            NC = B * KC
            v.wait_ge(*SCALAR["ctx rs"])
            chain(v.tensor_tensor(cnorm[:], lin(1)[0:64, 0:NC], rs[0:64, 0, 0:NC], ALU.mult))
            v.wait_ge(loaded["l1"], 16)
            chain(v.tensor_scalar(cnorm[:], cnorm[:], W["l1"]["a2_lny_g"], W["l1"]["a2_lny_b"], ALU.mult, ALU.add))
            chain(v.memset(base[:], 0.0))
            end_turn(v, VECTOR, 1)
            for g in ("x", "ctx", "l1f", "l2", "l3"):
                v.wait_ge(loaded[g], 16)

            with v.Fori(0, TURNS) as t:
                for u in U:
                    v.tensor_copy(cs[:, u, :], call[:, bass.ds((t * SLOTS + u) * KC, KC)])
                    v.tensor_copy(cn[:, u, :], cnorm[:, bass.ds((t * SLOTS + u) * KC, KC)])
                    v.tensor_copy(xs[:, u, :], xall[:, bass.ds((t * SLOTS + u) * S, S)])\
                        .then_inc(*VECTOR.did("begin", u))
                norm("l0x", lambda u: xn[:, u, :])
                for u in U:
                    v.wait_ge(*TENSOR["l0x q", u])
                    v.tensor_scalar(qT[:, u, 0, :], lin(u), W["l0"]["bq"], 8 ** -0.5, ALU.add, ALU.mult)\
                        .then_inc(*VECTOR.did("l0x", "q", u))
                context_kv("l0x", W["l0"]["bk"], 8)
                for u in U:
                    cross("l0x", u, 8, W["l0"]["bv"])
                for u in U:
                    v.wait_ge(*TENSOR["l0x y", u])
                    residual("l0x res", u, lin(u), 0, W["l0"]["bo"])
                for u in U:
                    v.wait_ge(*TENSOR["l0f xt", u])
                token_norm("l0f a", lambda u: aux(u))
                v.wait_ge(*VECTOR.last())
                token_norm("l0f b", lambda u: xn[:, u, :])
                for u in U:
                    v.wait_ge(*VECTOR.last())
                    x3 = xn[:, u, :].rearrange("p (i f) -> p i f", i=4)
                    g3 = W["l0"]["gammar"].unsqueeze(1).to_broadcast([128, 4, 128])
                    b3 = W["l0"]["betar"].unsqueeze(1).to_broadcast([128, 4, 128])
                    chain(v.tensor_tensor(x3, x3, g3, ALU.mult))
                    chain(v.tensor_tensor(x3, x3, b3, ALU.add))
                    quantise(u, x3, tq(u).rearrange("p (i f) -> p i f", i=4), wabs[:, 0:1], 50)\
                        .then_inc(*VECTOR.did("l0f q1", u))
                for u in U:
                    v.wait_ge(*TENSOR["l0f q1T", u])
                    v.tensor_copy(xq(u), aux(u).bitcast(BF16)[:, 0:512]).then_inc(*VECTOR.did("l0f xq", u))
                for u in U:
                    for i in range(4):
                        v.wait_ge(*TENSOR["l0f h", u, i])
                        v.scalar_tensor_tensor(hid[u][:, i, :], scb(i), sm(u, 50 + i, 1), W["l0"]["b1r"], ALU.mult,
                                               ALU.add).then_inc(*VECTOR.did("l0f h", u, i))
                for u in U:
                    v.wait_ge(*SCALAR["l0f gelu", u])
                    quantise(u, hid[u], tq2(u).rearrange("p (i f) -> p i f", i=4), wabs[:, 1:2], 60)\
                        .then_inc(*VECTOR.did("l0f q2", u))
                for u in U:
                    for i in range(4):
                        if i == 0:
                            v.wait_ge(*TENSOR["l0f y", u, 3])
                        last = v.scalar_tensor_tensor(xn[:, u, 128 * i:128 * i + 128], lin(u)[:, 128 * i:128 * i + 128],
                                                      sm(u, 60 + i, 1), W["l0"]["b2r"], ALU.mult, ALU.add)
                        if i < 3:
                            last.then_inc(*VECTOR.did())
                    last.then_inc(*VECTOR.did("l0f yt", u))
                for u in U:
                    v.wait_ge(*TENSOR["l0f yT", u])
                    residual("l0f res", u, aux(u), 4)
                w = W["l1"]
                norm("l1o", lambda u: xn[:, u, :])
                norm("l1a", lambda u: x1[:, u, :])
                affine("l1 x1", lambda u: x1[:, u, :], lambda u: x1[:, u, :], w["ln1_g"], w["ln1_b"])
                norm("l1b", lambda u: xn[:, u, :])
                affine("a1 y", lambda u: x2[:, u, :], lambda u: xn[:, u, :], w["a1_lny_g"], w["a1_lny_b"])
                affine("a1 in", lambda u: xn[:, u, :], lambda u: xn[:, u, :], w["a1_lnx_g"], w["a1_lnx_b"])
                for u in U:
                    for c in range(4):
                        v.wait_ge(*TENSOR["a1 q", u, c])
                        v.tensor_scalar(qT[:, u, c, :], scb(c), 32 ** -0.5, None, ALU.mult)\
                            .then_inc(*VECTOR.did("a1 q", u, c))
                for u in U:
                    VECTOR.table["a1", "q", u] = VECTOR.table["a1 q", 1, 3]
                for u in U:
                    self_attention("a1", u, 32)
                for u in U:
                    v.wait_ge(*TENSOR["a1 li1", u])
                    v.scalar_tensor_tensor(x2[:, u, :], lin(u), w["a1_li1_b"], x1[:, u, :], ALU.add, ALU.add)\
                        .then_inc(*VECTOR.did("a1 x2", u))
                norm("a1n3", lambda u: xn[:, u, :])
                affine("a1m in", lambda u: xn[:, u, :], lambda u: xn[:, u, :], w["a1_ln3_g"], w["a1_ln3_b"])
                for u in U:
                    v.wait_ge(*TENSOR["a1m y", u])
                    chain(v.scalar_tensor_tensor(x2[:, u, :], lin(u), w["a1_li3_b"], x2[:, u, :], ALU.add, ALU.add))
                    v.tensor_tensor(x1[:, u, :], x1[:, u, :], x2[:, u, :], ALU.add).then_inc(*VECTOR.did("a1 x1", u))
                norm("l1c", lambda u: x1[:, u, :])
                affine("l1c x1", lambda u: x1[:, u, :], lambda u: x1[:, u, :], w["ln2_g"], w["ln2_b"])
                norm("l1d", lambda u: xn[:, u, :])
                affine("a2 in", lambda u: xn[:, u, :], lambda u: xn[:, u, :], w["a2_lnx_g"], w["a2_lnx_b"])
                for u in U:
                    for c in range(4):
                        v.wait_ge(*TENSOR["a2 q", u, c])
                        v.tensor_scalar(qT[:, u, c, :], scb(c), 32 ** -0.5, None, ALU.mult)\
                            .then_inc(*VECTOR.did("a2 q", u, c))
                for u in U:
                    VECTOR.table["a2", "q", u] = VECTOR.table["a2 q", 1, 3]
                context_kv("a2", None, 32)
                for u in U:
                    cross("a2", u, 32, None)
                for u in U:
                    v.wait_ge(*TENSOR["a2 li1", u])
                    v.scalar_tensor_tensor(x2[:, u, :], lin(u), w["a2_li1_b"], x1[:, u, :], ALU.add, ALU.add)\
                        .then_inc(*VECTOR.did("a2 x2", u))
                norm("a2n3", lambda u: xn[:, u, :])
                affine("a2m in", lambda u: xn[:, u, :], lambda u: xn[:, u, :], w["a2_ln3_g"], w["a2_ln3_b"])
                for u in U:
                    v.wait_ge(*TENSOR["a2m y", u])
                    chain(v.scalar_tensor_tensor(x2[:, u, :], lin(u), w["a2_li3_b"], x2[:, u, :], ALU.add, ALU.add))
                    chain(v.tensor_tensor(x1[:, u, :], x1[:, u, :], x2[:, u, :], ALU.add))
                    residual("l1 res", u, x1[:, u, :], 1)
                w = W["l1f"]
                norm("l1f", lambda u: x1[:, u, :])
                for u in U:
                    v.wait_ge(*TENSOR["l1f q", u])
                    v.tensor_scalar(qT[:, u, 0, :], lin(u), w["bq"], 128 ** -0.5, ALU.add, ALU.mult)\
                        .then_inc(*VECTOR.did("l1f", "q", u))
                for u in U:
                    v.wait_ge(*TENSOR["l1f v", u])
                    for k in range(4):
                        last = v.tensor_tensor(vt[:, :, 128 * k:128 * k + 128],
                                               scb(1).rearrange("p (j f) -> p j f", j=4),
                                               K["col8"][:, 128 * k:128 * k + 128].unsqueeze(1).to_broadcast([128, 4, 128]),
                                               ALU.mult)
                    last.then_inc(*VECTOR.did("l1f v", u))
                    self_attention("l1f", u, 8)
                    VECTOR.table["l1f e0", u] = VECTOR.table["l1f", "nrm", u, 15]
                    v.wait_ge(*TENSOR["l1f tail", u])
                    v.tensor_tensor(rs[0:16, u, 0:384].rearrange("p (i f) -> p i f", i=3),
                                    scb(0)[0:16, 0:384].rearrange("p (i f) -> p i f", i=3),
                                    K["head16"][0:16, :].unsqueeze(1).to_broadcast([16, 3, 128]), ALU.mult)
                    v.tensor_copy(sq[0:16, u, 0:384], scb(1)[0:16, 0:384]).then_inc(*VECTOR.did("l1f tail", u))
                    v.wait_ge(*TENSOR["l1f o", u])
                    v.tensor_scalar(x2[:, u, :], lin(u), w["bv"], None, ALU.add).then_inc(*VECTOR.did("l1f o", u))
                for u in U:
                    v.wait_ge(*TENSOR["l1f logits", u])
                    lgv, hv, mx = view(u, 0, E1), view(u, 192, E1), sm(u, 256, 4)
                    chain(v.tensor_tensor(lgv, aux(u)[:, 0:64].rearrange("p (i e) -> p i e", i=4)[:, :, 0:E1],
                                          w["bswr"].unsqueeze(1).to_broadcast([128, 4, E1]), ALU.add))
                    chain(v.tensor_reduce(mx, lgv, AX.X, ALU.max))
                    chain(v.tensor_tensor(lgv, lgv, bc(mx, E1), ALU.subtract))
                    pick_first(hv, lgv, sm(u, 260, 4), E1).then_inc(*VECTOR.did("l1f hot", u))
                    VECTOR.table["l1f sub", u] = VECTOR.n
                for u in U:
                    lgv, hv = view(u, 0, E1), view(u, 192, E1)
                    cw9 = view(u, 64, 9)
                    v.wait_ge(*TENSOR["l1f count", u])
                    v.wait_ge(*SCALAR["l1f e", u])
                    s, rp, kept = sm(u, 256, 4), sm(u, 264, 4), sm(u, 268, 4)
                    chain(v.tensor_reduce(s, lgv, AX.X, ALU.add))
                    chain(v.reciprocal(rp, s))
                    cnt = view(u, 128, E1)
                    chain(v.tensor_tensor(cnt, aux(u)[:, 0:64].rearrange("p (i e) -> p i e", i=4)[:, :, 0:E1],
                                          base[:].unsqueeze(1).to_broadcast([128, 4, E1]), ALU.add))
                    chain(v.scalar_tensor_tensor(cnt, cnt, float(CAP), hv, ALU.is_lt, ALU.mult))
                    chain(v.tensor_reduce(kept, cnt, AX.X, ALU.add))
                    v.tensor_tensor(cw9[:, :, 0:E1], cnt, bc(rp, E1), ALU.mult)
                    chain(v.tensor_scalar(kept, kept, -1.0, 1.0, ALU.mult, ALU.add))
                    v.tensor_tensor(base[:], base[:], aux(u)[:, 64:64 + E1], ALU.add).then_inc(*VECTOR.did())
                    v.tensor_tensor(cw9[:, :, 8], kept, rp, ALU.mult).then_inc(*VECTOR.did("l1f cw", u))
                    v.wait_ge(*VECTOR.last())
                cw_turned("l1f", 9)
                for n in range(18):
                    e, u = n // 2, n % 2
                    v.wait_ge(*TENSOR["l1f rep", e, u])
                    if e >= 4:
                        v.wait_ge(*TENSOR["l1f expert", e - 4, u])
                    v.tensor_tensor(hid[u][:, e % 4, :], x2[:, u, :], scb(n % 4), ALU.mult)\
                        .then_inc(*VECTOR.did("l1f masked", e, u))
                for u in U:
                    v.wait_ge(*TENSOR["l1f expert", E1, u])
                    v.tensor_tensor(x2[:, u, :], lin(u), x1[:, u, :], ALU.add).then_inc(*VECTOR.did("l1f x2", u))
                norm("l1g", lambda u: xn[:, u, :])
                affine("l1g aff", lambda u: xn[:, u, :], lambda u: xn[:, u, :], w["gamma"], w["beta"])
                for u in U:
                    v.wait_ge(*VECTOR["l1g aff", u])
                    residual("l1f res", u, xn[:, u, :], 5)
                w = W["l2"]
                norm("l2x", lambda u: xn[:, u, :])
                for u in U:
                    v.wait_ge(*TENSOR["l2x q", u])
                    v.tensor_scalar(qT[:, u, 0, :], lin(u), w["bq"], None, ALU.add).then_inc(*VECTOR.did("l2x q", u))
                context_kv("l2x", w["bk"], 8)
                for u in U:
                    v.wait_ge(*TENSOR["l2x S", u])
                    softmax_sub(scb(u)[:, 0:4 * KC].rearrange("p (j k) -> p j k", j=4), pX(u)[:, 0], sm(u, 0, 4), 2)\
                        .then_inc(*VECTOR.did("l2x sub", u))
                for u in U:
                    v.wait_ge(*SCALAR["l2x exp", u])
                    s = sm(u, 4, 4)
                    chain(v.tensor_reduce(s, pX(u)[:, 0], AX.X, ALU.add))
                    chain(v.reciprocal(s, s))
                    v.tensor_tensor(pX(u)[:, 0], pX(u)[:, 0], bc(s, KC), ALU.mult).then_inc(*VECTOR.did("l2x nrm", u))
                for u in U:
                    v.wait_ge(*TENSOR["l2x y", u])
                    residual("l2x res", u, lin(u), 2, w["bv"])
                norm("l2f", lambda u: xn[:, u, :])
                for u in U:
                    v.wait_ge(*TENSOR["l2f logits", u])
                    lgv, hv, h2, mx = view(u, 0, E2), view(u, 192, E2), view(u, 128, E2), sm(u, 256, 4)
                    chain(v.tensor_tensor(lgv, aux(u)[:, 0:64].rearrange("p (i e) -> p i e", i=4)[:, :, 0:E2],
                                          w["rb2r"].unsqueeze(1).to_broadcast([128, 4, E2]), ALU.add))
                    chain(v.tensor_reduce(mx, lgv, AX.X, ALU.max))
                    chain(v.tensor_tensor(lgv, lgv, bc(mx, E2), ALU.subtract))
                    chain(pick_first(hv, lgv, sm(u, 260, 4), E2))
                    chain(v.scalar_tensor_tensor(view(u, 64, E2), hv, -BIG, lgv, ALU.mult, ALU.add))
                    chain(pick_first(h2, view(u, 64, E2), sm(u, 260, 4), E2))
                    v.tensor_tensor(hv, hv, h2, ALU.add).then_inc(*VECTOR.did("l2f sub", u))
                for u in U:
                    v.wait_ge(*SCALAR["l2f e", u])
                    lgv, hv, s = view(u, 0, E2), view(u, 192, E2), sm(u, 256, 4)
                    chain(v.tensor_reduce(s, lgv, AX.X, ALU.add))
                    chain(v.reciprocal(s, s))
                    chain(v.tensor_tensor(lgv, lgv, bc(s, E2), ALU.mult))
                    v.tensor_tensor(view(u, 64, E2), lgv, hv, ALU.mult).then_inc(*VECTOR.did("l2f cw", u))
                cw_turned("l2f", E2)
                experts("l2f", E2, w["be2"], lambda u: x2[:, u, :])
                for u in U:
                    v.wait_ge(*VECTOR["l2f out", E2 - 1, u])
                    residual("l2f res", u, x2[:, u, :], 6)
                norm("l3x", lambda u: xn[:, u, :])
                for u in U:
                    v.wait_ge(*TENSOR["l3x q", u])
                    v.tensor_scalar(qT[:, u, 0, :], lin(u), 8 ** -0.5, None, ALU.mult)\
                        .then_inc(*VECTOR.did("l3x", "q", u))
                context_kv("l3x", None, 8)
                for u in U:
                    cross("l3x", u, 8, None)
                for u in U:
                    v.wait_ge(*TENSOR["l3x y", u])
                    residual("l3x res", u, lin(u), 3)
                    v.wait_ge(*VECTOR.last())
                    v.tensor_copy(xall[:, bass.ds((t * SLOTS + u) * S, S)], xs[:, u, :])
                end_turn(v, VECTOR, t + 2)

            w = W["l3"]
            xrows = xall[:].rearrange("p (b s) -> p b s", b=B)
            with v.Fori(0, TURNS) as t:
                for u in U:
                    v.tensor_copy(rows(xs, u), xrows[:, :, bass.ds((t * SLOTS + u) * 128, 128)])\
                        .then_inc(*VECTOR.did("begin3", u))
                norm("l3f", lambda u: x1[:, u, :])
                for u in U:
                    for c in range(3):
                        v.wait_ge(*TENSOR["l3f qkv", u, c])
                        v.tensor_scalar(qT[:, u, c, :], scb(c), w["bqkv"][:, c:c + 1], None, ALU.add)\
                            .then_inc(*VECTOR.did("l3f qkv", u, c))
                v.wait_ge(*VECTOR.last())

                def prod(i, u):
                    q = rows4(qT[:, u, 0, :])
                    v.tensor_tensor(rows4(sq[:, u, :]), rows4(qT[:, u, 1, :]), q[:, i:i + 1, :].to_broadcast([128, 4, 128]),
                                    ALU.mult).then_inc(*VECTOR.did("l3f prod", u, i))

                for u in U:
                    prod(0, u)
                for i in range(4):
                    for u in U:
                        v.wait_ge(*TENSOR["l3f S", u, i])
                        m = x2[:, u, 0:128]
                        chain(v.tensor_reduce(m, aux(u).rearrange("p (j s) -> p s j", j=4), AX.X, ALU.max))
                        v.tensor_tensor(rows4(rs[:, u, :]), rows4(aux(u)), m.unsqueeze(1).to_broadcast([128, 4, 128]),
                                        ALU.subtract).then_inc(*VECTOR.did("l3f sub", u, i))
                        if i < 3:
                            prod(i + 1, u)
                    for u in U:
                        v.wait_ge(*SCALAR["l3f exp", u, i])
                        s, o = x2[:, u, 128:256], xn[:, u, 128 * i:128 * i + 128]
                        chain(v.tensor_reduce(s, rs[:, u, :].rearrange("p (j s) -> p s j", j=4), AX.X, ALU.add))
                        chain(v.reciprocal(s, s))
                        chain(v.tensor_tensor(rs[:, u, :], rs[:, u, :], qT[:, u, 2, :], ALU.mult))
                        chain(v.tensor_reduce(o, rs[:, u, :].rearrange("p (j s) -> p s j", j=4), AX.X, ALU.add))
                        v.tensor_tensor(o, o, s, ALU.mult).then_inc(*VECTOR.did("l3f o", u, i))
                for u in U:
                    v.wait_ge(*TENSOR["l3f y", u])
                    v.scalar_tensor_tensor(x2[:, u, :], lin(u), w["bo"], x1[:, u, :], ALU.add, ALU.add)\
                        .then_inc(*VECTOR.did("l3f x2", u))
                norm("l3g", lambda u: x1[:, u, :])
                affine("l3g aff", lambda u: x1[:, u, :], lambda u: x1[:, u, :], w["g1"], w["be1"])
                for u in U:
                    v.wait_ge(*TENSOR["l3f logits", u])
                    lgv = view(u, 0, E3)
                    chain(v.tensor_copy(lgv, aux(u)[:, 0:64].rearrange("p (i e) -> p i e", i=4)[:, :, 0:E3]))
                    pick_first(view(u, 64, E3), lgv, sm(u, 260, 4), E3).then_inc(*VECTOR.did("l3f cw", u))
                cw_turned("l3f", E3)
                experts("l3f", E3, w["b2"], lambda u: x2[:, u, :])
                for u in U:
                    v.wait_ge(*VECTOR["l3f out", E3 - 1, u])
                    v.tensor_tensor(x2[:, u, :], x1[:, u, :], x2[:, u, :], ALU.add).then_inc(*VECTOR.did("l3f z", u))
                norm("l3h", lambda u: xn[:, u, :])
                affine("l3h aff", lambda u: xn[:, u, :], lambda u: xn[:, u, :], w["g2"], w["be2"])
                for u in U:
                    v.wait_ge(*VECTOR["l3h aff", u])
                    residual("l3f res", u, xn[:, u, :], 7)
                    v.wait_ge(*VECTOR.last())
                    v.tensor_copy(xrows[:, :, bass.ds((t * SLOTS + u) * 128, 128)], rows(xs, u))
                end_turn(v, VECTOR, t + 2 + TURNS)


def build(trial, nc):
    tables = ({}, {}, {}, {})
    program(trial, *declare(trial), tables)
    program(nc, *declare(nc), tables)


def declare(nc):
    def arg(name, shape):
        return nc.dram_tensor(name, shape, F32, kind="ExternalInput").ap()

    packs = {g: arg("in_" + g, (128, sum(c for _, _, c in items))) for g, items in GROUPS.items()}
    return (arg("in_x", (128, B * S)), arg("in_ctx", (C, B * KC)), arg("in_const", (128, sum(n for _, n in CONST))),
            packs, arg("in_l2w", (128, 2 * E2 * 512)), arg("in_w1", (128, E3, 512)), arg("in_w2", (128, E3, 512)),
            nc.dram_tensor("out_0", (128, B * S), F32, kind="ExternalOutput").ap())


def layout(i):
    def col(a):
        return a.reshape(-1, 128).T if a.size > 64 else a.reshape(-1, 1)

    def chunk(a):
        return a.reshape(-1, 128, a.shape[-1]).transpose(1, 0, 2).reshape(128, -1)

    def row(a):
        return np.broadcast_to(a.reshape(1, -1), (128, a.size))

    g = {}
    p = {k[9:]: v for k, v in i.items() if k.startswith("L0_xattn_")}
    f = {k[7:]: v for k, v in i.items() if k.startswith("L0_ffn_")}
    g["l0"] = {"Wq": p["Wq"], "Wk": p["Wk"], "Wv": p["Wv"], "Wo": p["Wo"], "bq": col(p["bq"]), "bk": col(p["bk"]),
               "bv": col(p["bv"]), "bo": col(p["bo"]), "w1T": f["w1"].T, "w2T": chunk(f["w2"].T), "b1r": row(f["b1"]),
               "b2r": row(f["b2"]), "gammar": row(f["gamma"]), "betar": row(f["beta"])}
    p = {k[9:]: v for k, v in i.items() if k.startswith("L1_xattn_")}
    g["l1"] = {k: col(p[k]) for k in ("ln1_g", "ln1_b", "ln2_g", "ln2_b")}
    for a in ("a1_", "a2_"):
        for k in ("wq", "wk", "wv"):
            w = p[a + k]
            g["l1"][a + k] = w.transpose(1, 0, 2).reshape(w.shape[1], -1)
        g["l1"][a + "li1"], g["l1"][a + "li2"], g["l1"][a + "li3"] = (
            chunk(p[a + "li1_w"]), p[a + "li2_w"], chunk(p[a + "li3_w"]))
        for k in ("li1_b", "lnx_g", "lnx_b", "lny_g", "lny_b", "ln3_g", "ln3_b", "li2_b", "li3_b"):
            g["l1"][a + k] = col(p[a + k])
    p = {k[7:]: v for k, v in i.items() if k.startswith("L1_ffn_")}
    g["l1f"] = {k: p[k].reshape(128, 128).T for k in ("Wq", "Wk", "Wv")}
    g["l1f"].update({k: col(p[k]) for k in ("bq", "bk", "bv", "gamma", "beta")})
    g["l1f"].update({"We": p["We"].transpose(2, 0, 1).reshape(128, -1), "be": p["be"], "Wsw": p["Wsw"].T,
                     "bswr": row(p["bsw"])})
    p = {k[9:]: v for k, v in i.items() if k.startswith("L2_xattn_")}
    f = {k[7:]: v for k, v in i.items() if k.startswith("L2_ffn_")}
    g["l2"] = {"Wq": p["Wq"], "Wk": p["Wk"], "Wv": p["Wv"], "bq": col(p["bq"]), "bk": col(p["bk"]),
               "bv": col(p["bv"]), "rW1": f["rW1"], "rb1": col(f["rb1"]), "rW2": chunk(f["rW2"]),
               "rb2r": row(f["rb2"]), "be1": col(f["be1"]), "be2": f["be2"].T}
    l2w = np.concatenate([f["We1"].transpose(1, 0, 2).reshape(128, -1), chunk(f["We2"].reshape(E2 * 512, 128))], axis=1)
    p = {k[9:]: v for k, v in i.items() if k.startswith("L3_xattn_")}
    f = {k[7:]: v for k, v in i.items() if k.startswith("L3_ffn_")}
    g["l3"] = {"Wq": p["Wq"].T, "Wk": p["Wkv"][:128].T, "Wv": p["Wkv"][128:].T, "Wo": p["Wo"].T,
               "Wqkv": f["Wqkv"].T, "bqkv": col(f["bqkv"]), "Wo2": f["Wo"].T, "bo": col(f["bo"]), "g1": col(f["g1"]),
               "be1": col(f["be1"]), "g2": col(f["g2"]), "be2": col(f["be2"]), "Wg": f["Wg"].T, "b1": col(f["b1"]),
               "b2": f["b2"].T, "gates": row(np.concatenate([i["g_xattn"], i["g_ffn"]]))}
    out = {"in_l2w": l2w, "in_x": i["x"].reshape(B * S, D).T, "in_ctx": i["ctx_512"].reshape(B * KC, C).T,
           "in_w1": f["W1"].transpose(1, 0, 2), "in_w2": chunk(f["W2"].reshape(E3 * 512, 128)).reshape(128, E3, 512)}
    for name, items in GROUPS.items():
        parts = []
        for k, r, c in items:
            a = g[name][k]
            assert a.shape == (r, c), (name, k, a.shape)
            full = np.zeros((128, c), np.float32)
            full[:r] = a
            parts.append(full)
        out["in_" + name] = np.concatenate(parts, axis=1)
    table = const_table()
    out["in_const"] = np.concatenate([table[k] for k, _ in CONST], axis=1)
    return {k: np.ascontiguousarray(v) for k, v in out.items()}


def kernel(**inputs):
    import concourse.bacc as bacc
    from concourse.bass_utils import run_bass_kernel_spmd

    arrays = layout({k: np.asarray(v) for k, v in inputs.items()})
    trial, nc = (bacc.Bacc("TRN2", target_bir_lowering=False, num_devices=1) for _ in range(2))
    build(trial, nc)
    r = run_bass_kernel_spmd(nc, [arrays], core_ids=[0])
    return np.ascontiguousarray(r.results[0]["out_0"].T.reshape(B, S, D))
```
